# Optimizing a Trainium2 kernel written in Bass

```python
import numpy as np
import jax
import jax.numpy as jnp

def _softmax(x, axis=-1):
    return jax.nn.softmax(x, axis=axis)

def _gelu(x):
    return jax.nn.gelu(x, approximate=True)

def _silu(x):
    return jax.nn.silu(x)

def _sigmoid(x):
    return jax.nn.sigmoid(x)

def _layernorm(x, axis=-1, eps=1e-05):
    m = jnp.mean(x, axis=axis, keepdims=True)
    v = jnp.var(x, axis=axis, keepdims=True)
    return (x - m) / jnp.sqrt(v + eps)

def _scatter_add(tgt, idx, src, axis=0):
    return tgt.at[idx].add(src)

def _segment_sum(src, seg, n):
    return jax.ops.segment_sum(src, seg, n)
kernel_name = 'mk_seq_postln_d1_jaxref_r8_83fcb6'

def setup_inputs(seed: int=0):
    np.random.seed(seed)
    _w = jnp.asarray

    def _L0_attn_setup():
        import jax, jax.numpy as jnp
        import numpy as np
        HIDDEN = 256
        HEADS = 16
        HEAD_DIM = HIDDEN // HEADS
        B, S = (2, 256)
        key = jax.random.key(seed)
        ks = jax.random.split(key, 9)
        scale = 1.0 / np.sqrt(HIDDEN)
        inp = {'X': jax.random.normal(ks[0], (B, S, HIDDEN), dtype=jnp.float32), 'Wq': jax.random.normal(ks[1], (HIDDEN, HIDDEN), dtype=jnp.float32) * scale, 'bq': jax.random.normal(ks[2], (HIDDEN,), dtype=jnp.float32) * 0.01, 'Wk': jax.random.normal(ks[3], (HIDDEN, HIDDEN), dtype=jnp.float32) * scale, 'bk': jax.random.normal(ks[4], (HIDDEN,), dtype=jnp.float32) * 0.01, 'Wv': jax.random.normal(ks[5], (HIDDEN, HIDDEN), dtype=jnp.float32) * scale, 'bv': jax.random.normal(ks[6], (HIDDEN,), dtype=jnp.float32) * 0.01, 'Wo': jax.random.normal(ks[7], (HIDDEN, HIDDEN), dtype=jnp.float32) * scale, 'bo': jax.random.normal(ks[8], (HIDDEN,), dtype=jnp.float32) * 0.01}
        return inp
    _L0_attn_in = _L0_attn_setup()

    def _L0_ffn_setup():
        import jax, jax.numpy as jnp
        import numpy as np
        HIDDEN = 256
        INTER = 1024
        B, S = (4, 128)

        def _qmatmul(x, w_int8, scale):
            y = jnp.einsum('bsh,ho->bso', x, w_int8.astype(x.dtype))
            return y * scale
        key = jax.random.key(seed)
        ks = jax.random.split(key, 7)
        x = jax.random.normal(ks[0], (B, S, HIDDEN), dtype=jnp.float32)
        w_gate = jax.random.randint(ks[1], (HIDDEN, INTER), -128, 128, dtype=jnp.int32).astype(jnp.int8)
        w_up = jax.random.randint(ks[2], (HIDDEN, INTER), -128, 128, dtype=jnp.int32).astype(jnp.int8)
        w_down = jax.random.randint(ks[3], (INTER, HIDDEN), -128, 128, dtype=jnp.int32).astype(jnp.int8)
        s_gate = jax.random.uniform(ks[4], (INTER,), dtype=jnp.float32) * 0.02 + 0.001
        s_up = jax.random.uniform(ks[5], (INTER,), dtype=jnp.float32) * 0.02 + 0.001
        s_down = jax.random.uniform(ks[6], (HIDDEN,), dtype=jnp.float32) * 0.02 + 0.001
        return {'x': x, 'w_gate': w_gate, 'w_up': w_up, 'w_down': w_down, 's_gate': s_gate, 's_up': s_up, 's_down': s_down}
    _L0_ffn_in = _L0_ffn_setup()
    _d = {'L0_attn_X': _L0_attn_in['X'], 'L0_attn_Wq': _L0_attn_in['Wq'], 'L0_attn_bq': _L0_attn_in['bq'], 'L0_attn_Wk': _L0_attn_in['Wk'], 'L0_attn_bk': _L0_attn_in['bk'], 'L0_attn_Wv': _L0_attn_in['Wv'], 'L0_attn_bv': _L0_attn_in['bv'], 'L0_attn_Wo': _L0_attn_in['Wo'], 'L0_attn_bo': _L0_attn_in['bo'], 'L0_ffn_w_gate': _L0_ffn_in['w_gate'], 'L0_ffn_w_up': _L0_ffn_in['w_up'], 'L0_ffn_w_down': _L0_ffn_in['w_down'], 'L0_ffn_s_gate': _L0_ffn_in['s_gate'], 'L0_ffn_s_up': _L0_ffn_in['s_up'], 'L0_ffn_s_down': _L0_ffn_in['s_down']}
    _x0 = _d['L0_attn_X']
    _d['L0_attn_X'] = jax.random.normal(jax.random.fold_in(jax.random.key(seed), 1), (1, 2048, 256), dtype=_x0.dtype)
    del _x0
    return _d

def reference(L0_attn_X, L0_attn_Wq, L0_attn_bq, L0_attn_Wk, L0_attn_bk, L0_attn_Wv, L0_attn_bv, L0_attn_Wo, L0_attn_bo, L0_ffn_w_gate, L0_ffn_w_up, L0_ffn_w_down, L0_ffn_s_gate, L0_ffn_s_up, L0_ffn_s_down):

    def _L0_attn_ref(X, Wq, bq, Wk, bk, Wv, bv, Wo, bo):
        import jax, jax.numpy as jnp
        import numpy as np
        HIDDEN = 256
        HEADS = 16
        HEAD_DIM = HIDDEN // HEADS
        B, S = (2, 256)
        b, s, _ = X.shape
        Q = X @ Wq + bq
        K = X @ Wk + bk
        V = X @ Wv + bv
        q = Q.reshape(b, s, HEADS, HEAD_DIM).transpose(0, 2, 1, 3)
        k = K.reshape(b, s, HEADS, HEAD_DIM).transpose(0, 2, 1, 3)
        v = V.reshape(b, s, HEADS, HEAD_DIM).transpose(0, 2, 1, 3)
        scores = jnp.einsum('bhqd,bhkd->bhqk', q, k) / np.sqrt(HEAD_DIM)
        attn = jax.nn.softmax(scores, axis=-1)
        out = jnp.einsum('bhqk,bhkd->bhqd', attn, v)
        out = out.transpose(0, 3, 2, 1).reshape(b, s, HEADS * HEAD_DIM)
        return out @ Wo + bo

    def _L0_ffn_ref(x, w_gate, w_up, w_down, s_gate, s_up, s_down):
        import jax, jax.numpy as jnp
        import numpy as np
        HIDDEN = 256
        INTER = 1024
        B, S = (4, 128)

        def _qmatmul(x, w_int8, scale):
            y = jnp.einsum('bsh,ho->bso', x, w_int8.astype(x.dtype))
            return y * scale
        gate = jax.nn.silu(_qmatmul(x, w_gate, s_gate))
        up = _qmatmul(x, w_up, s_up)
        fuse = gate * up
        return _qmatmul(fuse, w_down, s_down)
    x = L0_attn_X
    x = _layernorm(x + _L0_attn_ref(x, L0_attn_Wq, L0_attn_bq, L0_attn_Wk, L0_attn_bk, L0_attn_Wv, L0_attn_bv, L0_attn_Wo, L0_attn_bo), axis=-1)
    x = _layernorm(x + _L0_ffn_ref(x, L0_ffn_w_gate, L0_ffn_w_up, L0_ffn_w_down, L0_ffn_s_gate, L0_ffn_s_up, L0_ffn_s_down), axis=-1)
    return x

_drawn_inputs = setup_inputs


def setup_inputs(seed=0):
    import zlib

    import numpy as np

    out = dict(_drawn_inputs(seed))
    spreads = {}
    factors = {'L0_attn_bq': 55.313, 'L0_attn_bk': 64.0, 'L0_attn_bv': 3.789, 'L0_attn_bo': 4.056}
    for name, (base, spread) in spreads.items():
        noise = np.random.default_rng([zlib.crc32(name.encode()), seed]).standard_normal(out[name].shape)
        drawn = base * np.exp(spread * noise) if base else spread * noise
        out[name] = jnp.asarray(drawn.astype(out[name].dtype))
    for name, factor in factors.items():
        out[name] = (out[name] * factor).astype(out[name].dtype)
    return out
```

```python
import numpy as np
import concourse.bass as bass
from concourse import mybir
from contextlib import ExitStack


def layer_program(nc, X, Wq, bq, Wk, bk, Wv, bv, Wo, bo, w_gate, w_up, w_down, s_gate, s_up, s_down, out):
    f32, f32r, bf16 = mybir.dt.float32, mybir.dt.float32r, mybir.dt.bfloat16
    i8, i32 = mybir.dt.int8, mybir.dt.int32
    ALU = mybir.AluOpType
    ACT = mybir.ActivationFunctionType
    AXX = mybir.AxisListType.X
    MAX_ACROSS = bass.bass_isa.ReduceOp.max

    P = 128
    S, HID = X.shape[1], X.shape[2]
    NH = 16
    HD = HID // NH
    INTER = s_gate.shape[0]
    KO = HID // P
    TT = S // P
    CW = 512
    CH = S // CW
    TPC = TT // CH
    MT = INTER // P
    HPB = P // HD
    NPROD = 6
    SROW = NPROD * HD
    ROWS = SROW + 3
    Q_PART = [0, 0, 0, 1, 1, 2]
    K_PART = [0, 1, 2, 0, 1, 0]
    VW = 32
    NSLOT = 3
    SCALE = float(HD) ** -0.5
    SAFE = 40.0
    EPS = 1e-5

    with ExitStack() as ctx:
        arena_at = (nc.sbuf_base + 63) // 64 * 64
        place_at = [arena_at]

        def place(name, shape, dt, at=None):
            size = int(np.prod(shape[1:])) * {f32: 4, f32r: 4, i32: 4, bf16: 2, i8: 1}[dt]
            where = place_at[0] if at is None else at
            if at is None:
                place_at[0] += (size + 63) // 64 * 64
            return nc.alloc_sbuf_tensor_at(name, shape, dt, offset=where)

        def region(size):
            at = place_at[0]
            place_at[0] += size
            return at

        KB = 1024
        x_tok = place("x_tok", [P, TT, HID], f32)
        gate8 = place("gate8", [P, KO, INTER // 4], i32)
        up8 = place("up8", [P, KO, INTER // 4], i32)
        down8 = place("down8", [P, MT, HID // 4], i32)
        wo_hi = place("wo_hi", [P, KO, HID], f32r)
        wo_lo = place("wo_lo", [P, KO, HID], f32r)
        ident = place("ident", [P, P], f32)
        head_sum = place("head_sum", [P, 32], bf16)
        bq_c = place("bq_c", [P, KO], f32)
        bk_c = place("bk_c", [P, KO], f32)
        bv_b = place("bv_b", [P, 2, HID], f32)
        bo_b = place("bo_b", [P, 2, HID], f32)
        sdown_b = place("sdown_b", [P, HID], f32)
        sgate_c = place("sgate_c", [P, MT], f32)
        sup_c = place("sup_c", [P, MT], f32)
        norm_max = place("norm_max", [P, 4], f32)
        norm_qk = place("norm_qk", [P, 2], f32)
        norm_all = place("norm_all", [P, 2], f32)
        norm_sum = place("norm_sum", [P, 1], f32)
        shift_neg = place("shift_neg", [P, 1], f32)
        exact_flag = place("exact_flag", [P, 1], i32)
        row_max = place("row_max", [P, NH, TT], f32)
        shift = place("shift", [P, 3, 2 * P], bf16)
        shift_rest = place("shift_rest", [P, 2 * P], f32)
        den = place("den", [P, 2, 16], f32)
        stats = place("stats", [P, TT, 6], f32)
        stats_c = place("stats_c", [P, TPC, 6], f32)
        mean_var = place("mean_var", [P, TT, 2], f32)
        std = place("std", [P, TT], f32)
        rstd = place("rstd", [P, TT], f32)
        eps_c = place("eps_c", [P, 1], f32)
        q_stack = [place(f"q_stack{i}", [ROWS, S], bf16) for i in range(NSLOT)]
        k_stack = [place(f"k_stack{i}", [ROWS, S], bf16) for i in range(NSLOT)]
        v_slot = [place(f"v_slot{i}", [P, TT, VW], f32) for i in range(NSLOT)]

        at = region(16 * KB)
        v_all = place("v_all", [P, TT, HID], f32, at)
        wd = place("wd", [P, MT, HID], f32r, at)
        h32 = place("h32", [P, 2, CW], f32, at + 8 * KB)
        sg = place("sg", [P, 2, CW], f32, at + 12 * KB)
        at = region(40 * KB)
        w_raw = place("w_raw", [P, 4, KO * HID], f32, at)
        w_hi = place("w_hi", [P, 3, KO, HID], f32r, at + 8 * KB)
        w_lo = place("w_lo", [P, 3, KO, HID], f32r, at + 14 * KB)
        rest = place("rest", [P, 2, CW], f32, at + 20 * KB)
        squares = place("squares", [P, 4, S], bf16, at + 24 * KB)
        attn = place("attn", [P, S // NH // 4, NH, NH], f32, at)
        h_hi = place("h_hi", [P, MT, CW], f32r, at)
        h_lo = place("h_lo", [P, MT, CW], f32r, at + 16 * KB)
        z_tmp = place("z_tmp", [P, 2, HID], f32, at + 32 * KB)
        r_tmp = place("r_tmp", [P, TPC, HID], f32, at + 34 * KB)
        at = region(48 * KB)
        q_parts = place("q_parts", [P, KO, 3, S], bf16, at)
        k_parts = place("k_parts", [P, KO, 3, S], bf16, at + 24 * KB)
        at_hi = place("at_hi", [P, KO, S], f32r, at)
        at_lo = place("at_lo", [P, KO, S], f32r, at + 16 * KB)
        wg = place("wg", [P, KO, INTER], f32r, at + 32 * KB)
        wu = place("wu", [P, KO, INTER], f32r, at + 40 * KB)
        at = region(32 * KB)
        xt_hi = place("xt_hi", [P, KO, S], f32r, at)
        xt_lo = place("xt_lo", [P, KO, S], f32r, at + 16 * KB)
        probs = place("probs", [P, 3, CH, CW], f32, at)
        at32 = place("at32", [P, KO, HD, 4, 32], f32, at)
        yt_hi = place("yt_hi", [P, KO, S], f32r, at)
        yt_lo = place("yt_lo", [P, KO, S], f32r, at + 16 * KB)

        ps = ctx.enter_context(nc.psum_tensor("ps", [P, 8, CW], f32))
        ACC = 6

        def sem(name):
            return ctx.enter_context(nc.semaphore(name))

        x_loaded = [sem(f"x_loaded{c}") for c in range(CH)]
        w_loaded = [sem(f"w_loaded{i}") for i in range(4)]
        bias_loaded = sem("bias_loaded")
        late_loaded = sem("late_loaded")
        consts_ready = sem("consts_ready")
        pool_step = sem("pool_step")
        dve_step = sem("dve_step")
        pad_ready = sem("pad_ready")
        w_hi_ready = sem("w_hi_ready")
        w_ready = sem("w_ready")
        xt_psum = sem("xt_psum")
        xt_hi_ready = sem("xt_hi_ready")
        xt_ready = sem("xt_ready")
        proj_psum = sem("proj_psum")
        part1_ready = sem("part1_ready")
        squares_ready = sem("squares_ready")
        rest_ready = sem("rest_ready")
        part2_ready = sem("part2_ready")
        part3_ready = sem("part3_ready")
        v_ready = sem("v_ready")
        norms_psum = sem("norms_psum")
        norms_ready = sem("norms_ready")
        norms_reduced = sem("norms_reduced")
        flag_ready = sem("flag_ready")
        gen_loaded = sem("gen_loaded")
        gen_scores = sem("gen_scores")
        gen_max = sem("gen_max")
        gen_turned = sem("gen_turned")
        gen_split = sem("gen_split")
        gen_reloaded = sem("gen_reloaded")
        shift_ready = sem("shift_ready")
        stack_loaded = [sem(f"stack_loaded{i}") for i in range(NSLOT)]
        v_slot_ready = sem("v_slot_ready")
        scores_ready = sem("scores_ready")
        exp_done = sem("exp_done")
        pv_done = sem("pv_done")
        attn_saved = sem("attn_saved")
        ffn_w_ready = sem("ffn_w_ready")
        bo_added = sem("bo_added")
        attn_turned = sem("attn_turned")
        den_ready = sem("den_ready")
        attn_scaled = sem("attn_scaled")
        at_hi_ready = sem("at_hi_ready")
        at_ready = sem("at_ready")
        wo_psum = sem("wo_psum")
        ln1_sum = sem("ln1_sum")
        ln1_var = sem("ln1_var")
        ln1_std = sem("ln1_std")
        ln1_ready = sem("ln1_ready")
        yt_psum = sem("yt_psum")
        yt_hi_ready = sem("yt_hi_ready")
        yt_ready = sem("yt_ready")
        gate_up_psum = sem("gate_up_psum")
        gate_up_free = sem("gate_up_free")
        silu_done = sem("silu_done")
        h_hi_ready = sem("h_hi_ready")
        h_ready = sem("h_ready")
        down_psum = sem("down_psum")
        down_free = sem("down_free")
        z_ready = sem("z_ready")
        ln2_sum = sem("ln2_sum")
        ln2_stats = sem("ln2_stats")
        ln2_saved = sem("ln2_saved")
        ln2_var = sem("ln2_var")
        ln2_std = sem("ln2_std")
        ln2_rstd = sem("ln2_rstd")
        ln2_ready = sem("ln2_ready")
        stored = sem("stored")

        block = ctx.enter_context(nc.Block())

        x_view = X.rearrange("a (t p) n -> p (a t) n", p=P)
        out_view = out.rearrange("a (t p) n -> p (a t) n", p=P)
        STACK = 16 * 2 * NPROD
        SHIFT = 16 * 3

        UNITS = [(c, k) for c in range(CH) for k in range(6)]
        QK = [u for u in UNITS if u[1] < 4]

        def qk_before(n):
            return sum(1 for u in UNITS[:n] if u[1] < 4)

        def v_before(n):
            return n - qk_before(n)

        @block.sync
        def _(sp):
            for c in range(CH):
                sp.dma_start(x_tok[:, TPC * c:TPC * (c + 1), :], x_view[:, TPC * c:TPC * (c + 1), :]
                             ).then_inc(x_loaded[c], 16)
            sp.dma_start(gate8[:], w_gate.rearrange("(k p) n -> p k n", p=P)).then_inc(late_loaded, 16)
            sp.dma_start(up8[:], w_up.rearrange("(k p) n -> p k n", p=P)).then_inc(late_loaded, 16)
            sp.dma_start(down8[:], w_down.rearrange("(k p) n -> p k n", p=P)).then_inc(late_loaded, 16)

            def load_stack(h, slot, done):
                block_of_head, row = h // HPB, HD * (h % HPB)
                for parts, stack, which in ((q_parts, q_stack[slot], Q_PART), (k_parts, k_stack[slot], K_PART)):
                    for j in range(NPROD):
                        sp.dma_start(stack[HD * j:HD * (j + 1), :],
                                     parts[row:row + HD, block_of_head, which[j], :]).then_inc(done, 16)

            def load_shift(h, slot):
                for i in range(3):
                    sp.dma_start(q_stack[slot][SROW + i:SROW + i + 1, :],
                                 shift[h * HPB:(h + 1) * HPB, i, :]).then_inc(stack_loaded[slot], 16)

            def refill(h, slot):
                sp.wait_ge(scores_ready, (h - NSLOT + 1) * 2 * TT)
                load_stack(h, slot, stack_loaded[slot])
                load_shift(h, slot)

            sp.wait_ge(part1_ready, len(QK))
            sp.wait_ge(part2_ready, len(QK))
            sp.wait_ge(part3_ready, len(QK))
            for h in range(NSLOT):
                load_stack(h, h, stack_loaded[h])
            sp.wait_ge(flag_ready, 1)
            need_exact = sp.value_load(exact_flag[0:1, 0:1], min_val=0, max_val=1)
            with sp.If(need_exact > 0):
                for s in range(NSLOT):
                    sp.wait_ge(stack_loaded[s], STACK)
                for h in range(NH):
                    if h:
                        sp.wait_ge(gen_max, h * TT + 2)
                    load_stack(h, 0, gen_loaded)
                sp.wait_ge(gen_max, NH * TT + 2)
                load_stack(0, 0, gen_reloaded)
                sp.wait_ge(gen_reloaded, STACK)
            sp.wait_ge(shift_ready, 1)
            for h in range(NSLOT):
                load_shift(h, h)
            for h in range(NSLOT, NH):
                refill(h, h % NSLOT)
            for c in range(CH):
                sp.wait_ge(ln2_ready, TPC * (c + 1))
                sp.dma_start(out_view[:, TPC * c:TPC * (c + 1), :], x_tok[:, TPC * c:TPC * (c + 1), :]
                             ).then_inc(stored, 16)
            sp.wait_ge(stored, 16 * CH)

        @block.gpsimd
        def _(pool):
            steps = [0]

            def then(instruction):
                steps[0] += 1
                instruction.then_inc(pool_step, 1)
                pool.wait_ge(pool_step, steps[0])

            then(nc.gpsimd.memset(ident[:], 0.0))
            nc.gpsimd.affine_select(out=ident[:], in_=ident[:], compare_op=ALU.not_equal, fill=1.0, base=0,
                                    pattern=[[-1, P]], channel_multiplier=1).then_inc(consts_ready, 1)
            then(nc.gpsimd.memset(head_sum[:], 1.0))
            then(nc.gpsimd.affine_select(out=head_sum[:], in_=head_sum[:], compare_op=ALU.is_ge, fill=0.0, base=0,
                                         pattern=[[-HD, 32]], channel_multiplier=1))
            nc.gpsimd.affine_select(out=head_sum[:], in_=head_sum[:], compare_op=ALU.is_ge, fill=0.0, base=HD - 1,
                                    pattern=[[HD, 32]], channel_multiplier=-1).then_inc(consts_ready, 1)
            for s in range(NSLOT):
                then(nc.gpsimd.memset(v_slot[s][:], 0.0))
                nc.gpsimd.memset(v_slot[s][:, :, HD:HD + 1], 1.0).then_inc(pad_ready, 1)
            for n, (c, k) in enumerate(QK):
                parts = q_parts if k < 2 else k_parts
                pool.wait_ge(rest_ready, n + 1)
                nc.gpsimd.tensor_copy(parts[:, k % 2, 1, c * CW:(c + 1) * CW], rest[:, n % 2, :]
                                      ).then_inc(part2_ready, 1)
            pool.wait_ge(norms_ready, 1)
            nc.gpsimd.partition_all_reduce(norm_all[:], norm_qk[:], P, MAX_ACROSS).then_inc(norms_reduced, 1)
            pool.wait_ge(bias_loaded, 16 * 9)
            pool.wait_ge(xt_ready, 2 * CH)
            for t in range(0, TT, 2):
                nc.gpsimd.tensor_tensor(x_tok[:, t:t + 2, :], x_tok[:, t:t + 2, :], bo_b[:], ALU.add
                                        ).then_inc(bo_added, 1)
            pool.wait_ge(late_loaded, 16 * 3)
            pool.wait_ge(scores_ready, NH * 2 * TT)
            nc.gpsimd.tensor_copy(wg[:], gate8[:].bitcast(i8)).then_inc(ffn_w_ready, 1)
            nc.gpsimd.tensor_copy(wu[:], up8[:].bitcast(i8)).then_inc(ffn_w_ready, 1)
            pool.wait_ge(v_slot_ready, NH)
            nc.gpsimd.tensor_copy(wd[:], down8[:].bitcast(i8)).then_inc(ffn_w_ready, 1)

        def three_heads(engine, head):
            head(0, 0)
            with engine.Fori(0, (NH - 1) // 3) as i:
                for j in range(1, 4):
                    head(i * 3 + j, j)

        @block.scalar
        def _(act):
            for i, w in enumerate((Wq, Wk, Wv, Wo)):
                act.dma_start(w_raw[:, i, :].rearrange("p (k n) -> p k n", k=KO),
                              w.rearrange("(k p) n -> p k n", p=P)).then_inc(w_loaded[i], 16)
            act.dma_start(bq_c[:], bq.rearrange("(k p) -> p k", p=P),
                          allow_slow_non_contiguous=True).then_inc(bias_loaded, 16)
            act.dma_start(bk_c[:], bk.rearrange("(k p) -> p k", p=P),
                          allow_slow_non_contiguous=True).then_inc(bias_loaded, 16)
            for i in range(2):
                act.dma_start(bv_b[:, i, :], bv.partition_broadcast(P)).then_inc(bias_loaded, 16)
                act.dma_start(bo_b[:, i, :], bo.partition_broadcast(P)).then_inc(bias_loaded, 16)
            act.dma_start(sdown_b[:], s_down.partition_broadcast(P)).then_inc(bias_loaded, 16)
            act.dma_start(sgate_c[:], s_gate.rearrange("(k p) -> p k", p=P),
                          allow_slow_non_contiguous=True).then_inc(bias_loaded, 16)
            act.dma_start(sup_c[:], s_up.rearrange("(k p) -> p k", p=P),
                          allow_slow_non_contiguous=True).then_inc(bias_loaded, 16)
            for i in range(4):
                act.wait_ge(w_loaded[i], 16)
                dst = w_hi[:, i, :, :] if i < 3 else wo_hi[:]
                nc.scalar.copy(dst, w_raw[:, i, :].rearrange("p (k n) -> p k n", k=KO)).then_inc(w_hi_ready, 1)
            for t in range(KO * CH):
                c, ko = t // KO, t % KO
                act.wait_ge(xt_psum, t + 1)
                nc.scalar.copy(xt_hi[:, ko, c * CW:(c + 1) * CW], ps[:, t, :]).then_inc(xt_hi_ready, 1)
            act.wait_ge(bias_loaded, 16 * 9)
            for n, (c, k) in enumerate(UNITS):
                if k < 4:
                    parts, b_c = (q_parts, bq_c) if k < 2 else (k_parts, bk_c)
                    act.wait_ge(proj_psum, n + 1)
                    nc.scalar.activation(parts[:, k % 2, 0, c * CW:(c + 1) * CW], ps[:, n % 8, :], ACT.Identity,
                                         bias=b_c[:, k % 2:k % 2 + 1]).then_inc(part1_ready, 1)
                    nc.scalar.activation(squares[:, k, c * CW:(c + 1) * CW], ps[:, n % 8, :], ACT.Square,
                                         bias=b_c[:, k % 2:k % 2 + 1]).then_inc(squares_ready, 1)

            def head(h, j):
                for kt in range(TT):
                    u = h * TT + kt
                    for half in range(2):
                        ring = (2 * (j * TT + kt) + half) % 3
                        act.wait_ge(scores_ready, 2 * u + half + 1)
                        if half == 0 and not (j == 0 and kt < 3):
                            act.wait_ge(pv_done, u - 2)
                        nc.scalar.activation(
                            probs[:, (j * TT + kt) % 3, 2 * half:2 * half + 2, :].rearrange("p a b -> p (a b)"),
                            ps[:, 2 * ring:2 * ring + 2, :].rearrange("p a b -> p (a b)"),
                            ACT.Exp, bias=0.0, scale=SCALE).then_inc(exp_done, 1)

            act.wait_ge(xt_ready, 2 * CH)
            three_heads(act, head)

            for g in range(8):
                ko, q = g // 4, g % 4
                act.wait_ge(attn_scaled, 16)
                nc.scalar.copy(at_hi[:, ko, q * CW:(q + 1) * CW],
                               at32[:, ko, 4 * q:4 * q + 4, :, :].rearrange("p a b c -> p (a b c)")
                               ).then_inc(at_hi_ready, 1)
            act.wait_ge(ln1_var, TT)
            nc.scalar.activation(std[:], mean_var[:, :, 1], ACT.Sqrt, bias=eps_c[:]).then_inc(ln1_std, 1)
            for t in range(KO * CH):
                c, ko = t // KO, t % KO
                act.wait_ge(yt_psum, t + 1)
                nc.scalar.copy(yt_hi[:, ko, c * CW:(c + 1) * CW], ps[:, t, :]).then_inc(yt_hi_ready, 1)
            with act.Fori(0, CH) as c:
                for m in range(MT + 1):
                    if m < MT:
                        u = c * MT + m
                        act.wait_ge(gate_up_psum, u + 1)
                        act.wait_ge(gate_up_free, u + 1)
                        nc.scalar.activation(sg[:, m % 2, :], ps[:, m % 2, :], ACT.Silu,
                                             scale=sgate_c[:, m:m + 1]).then_inc(silu_done, 1)
                    if m > 0:
                        act.wait_ge(gate_up_free, c * MT + m + 2)
                        nc.scalar.copy(h_hi[:, m - 1, :], h32[:, (m - 1) % 2, :]).then_inc(h_hi_ready, 1)
            act.wait_ge(ln2_var, TT)
            nc.scalar.activation(std[:], mean_var[:, :, 1], ACT.Sqrt, bias=eps_c[:]).then_inc(ln2_std, 1)

        @block.vector
        def _(dve):
            steps = [0]

            def then(instruction):
                steps[0] += 1
                instruction.then_inc(dve_step, 1)
                dve.wait_ge(dve_step, steps[0])

            then(nc.vector.memset(eps_c[:], EPS))
            then(nc.vector.memset(shift[:], 0.0))
            for s in range(NSLOT):
                nc.vector.memset(k_stack[s][SROW:ROWS, :], 1.0).then_inc(pad_ready, 1)
            for i in range(4):
                dst, hi = (w_lo[:, i, :, :], w_hi[:, i, :, :]) if i < 3 else (wo_lo[:], wo_hi[:])
                dve.wait_ge(w_hi_ready, i + 1)
                nc.vector.tensor_tensor(dst, w_raw[:, i, :].rearrange("p (k n) -> p k n", k=KO), hi.bitcast(f32),
                                        ALU.subtract).then_inc(w_ready, 1)
            for t in range(KO * CH):
                c, ko = t // KO, t % KO
                dve.wait_ge(xt_hi_ready, t + 1)
                nc.vector.tensor_tensor(xt_lo[:, ko, c * CW:(c + 1) * CW], ps[:, t, :],
                                        xt_hi[:, ko, c * CW:(c + 1) * CW].bitcast(f32), ALU.subtract
                                        ).then_inc(xt_ready, 1)
            dve.wait_ge(bias_loaded, 16 * 9)

            def third_part(n):
                c, k = QK[n]
                parts = q_parts if k < 2 else k_parts
                dve.wait_ge(part2_ready, n + 1)
                nc.vector.tensor_tensor(parts[:, k % 2, 2, c * CW:(c + 1) * CW], rest[:, n % 2, :],
                                        parts[:, k % 2, 1, c * CW:(c + 1) * CW], ALU.subtract
                                        ).then_inc(part3_ready, 1)

            for n, (c, k) in enumerate(UNITS):
                if k < 4:
                    parts, b_c = (q_parts, bq_c) if k < 2 else (k_parts, bk_c)
                    m = qk_before(n)
                    dve.wait_ge(squares_ready, m + 1)
                    if m >= 2:
                        dve.wait_ge(part3_ready, m - 1)
                    nc.vector.scalar_tensor_tensor(rest[:, m % 2, :], ps[:, n % 8, :], b_c[:, k % 2:k % 2 + 1],
                                                   parts[:, k % 2, 0, c * CW:(c + 1) * CW], ALU.add, ALU.subtract
                                                   ).then_inc(rest_ready, 1)
                    if m >= 1:
                        third_part(m - 1)
                else:
                    t = TPC * c + 2 * (k - 4)
                    dve.wait_ge(proj_psum, n + 1)
                    nc.vector.tensor_tensor(v_all[:, t:t + 2, :], ps[:, n % 8, :].rearrange("p (a b) -> p a b", a=2),
                                            bv_b[:], ALU.add).then_inc(v_ready, 1)
            third_part(len(QK) - 1)

            def fill_v_slot(h, slot):
                nc.vector.tensor_scalar(v_slot[slot][:, :, 0:HD], v_all[:, :, bass.ds(h * HD, HD)], 1.0, None,
                                        ALU.mult).then_inc(v_slot_ready, 1)

            dve.wait_ge(pad_ready, 2 * NSLOT)
            dve.wait_ge(v_ready, TT // 2)
            for h in range(NSLOT):
                fill_v_slot(h, h)

            dve.wait_ge(norms_psum, 1)
            then(nc.vector.reduce_max(norm_max[:], ps[:, 0:4, :], AXX))
            nc.vector.tensor_tensor(norm_qk[:], norm_max[:, 0:4:2], norm_max[:, 1:4:2], ALU.max
                                    ).then_inc(norms_ready, 1)
            dve.wait_ge(norms_reduced, 1)
            then(nc.vector.tensor_tensor(norm_sum[:], norm_all[:, 0:1], norm_all[:, 1:2], ALU.add))
            then(nc.vector.tensor_scalar(shift_neg[:], norm_sum[:], -0.51, None, ALU.mult))
            then(nc.vector.tensor_scalar(shift[:, 0, :], shift[:, 1, :], shift_neg[:, 0:1], None, ALU.add))
            then(nc.vector.tensor_scalar(norm_sum[:], norm_sum[:], 0.51 * SCALE, SAFE, ALU.mult, ALU.is_le))
            nc.vector.tensor_scalar(exact_flag[:], norm_sum[:], -1.0, 1.0, ALU.mult, ALU.add).then_inc(flag_ready, 1)
            dve.wait_ge(flag_ready, 1)
            need_exact = dve.value_load(exact_flag[0:1, 0:1], min_val=0, max_val=1)
            with dve.If(need_exact > 0):
                dve.sem_inc(gen_max, 2)
                with dve.Fori(0, NH) as h:
                    for t in range(TT):
                        dve.wait_ge(gen_scores, h * TT + t + 1)
                        nc.vector.reduce_max(row_max[:, bass.ds(h, 1), t], ps[:, 4 * (t % 2):4 * (t % 2) + 4, :]
                                             .rearrange("p a b -> p (a b)"), AXX).then_inc(gen_max, 1)
                dve.wait_ge(gen_turned, 2)
                turned = ps[:, 0, 0:2 * P]
                nc.vector.tensor_scalar(shift[:, 0, :], turned, -1.0, None, ALU.mult).then_inc(gen_split, 1)
                dve.wait_ge(gen_split, 1)
                nc.vector.scalar_tensor_tensor(shift_rest[:], turned, -1.0, shift[:, 0, :], ALU.mult, ALU.subtract
                                               ).then_inc(gen_split, 1)
                dve.wait_ge(gen_split, 2)
                nc.vector.tensor_copy(shift[:, 1, :], shift_rest[:]).then_inc(gen_split, 1)
                dve.wait_ge(gen_split, 3)
                nc.vector.tensor_tensor(shift[:, 2, :], shift_rest[:], shift[:, 1, :], ALU.subtract
                                        ).then_inc(gen_split, 1)
                dve.wait_ge(gen_split, 4)
            dve.sem_inc(shift_ready, 1)

            def head(h, j):
                dve.wait_ge(pv_done, (h + 1) * TT)
                nc.vector.tensor_scalar(attn[:, :, :, bass.ds(h, 1)],
                                        ps[:, ACC, :].rearrange("p (u r o) -> p u r o", r=NH, o=1), 1.0, None,
                                        ALU.mult).then_inc(attn_saved, 1)

            def head_and_fill(h, j):
                head(h, j)
                fill_v_slot(h + NSLOT, j % 3)

            head_and_fill(0, 0)
            with dve.Fori(0, (NH - 1) // 3 - 1) as i:
                for j in range(1, 4):
                    head_and_fill(i * 3 + j, j)
            for h in range(NH - NSLOT, NH):
                head(h, h)

            for g in range(16):
                ug, ko = g // 2, g % 2
                pst = ps[:, g % 6, :].rearrange("p (u j d) -> p u j d", u=4, d=32)
                dve.wait_ge(attn_turned, g + 1)
                if g >= 2:
                    dve.wait_ge(attn_scaled, g - 1)
                nc.vector.reciprocal(den[:, g % 2, :].rearrange("p (u j) -> p u j", u=4), pst[:, :, :, HD]
                                     ).then_inc(den_ready, 1)
                dve.wait_ge(den_ready, g + 1)
                nc.vector.tensor_tensor(
                    at32[:, ko, :, :, 4 * ug:4 * ug + 4].rearrange("p d j u -> p u j d"), pst[:, :, :, 0:HD],
                    den[:, g % 2, :].rearrange("p (u j o) -> p u j o", u=4, o=1).to_broadcast([P, 4, 4, HD]),
                    ALU.mult).then_inc(attn_scaled, 1)
            for g in range(8):
                ko, q = g // 4, g % 4
                dve.wait_ge(at_hi_ready, g + 1)
                nc.vector.tensor_tensor(at_lo[:, ko, q * CW:(q + 1) * CW],
                                        at32[:, ko, 4 * q:4 * q + 4, :, :].rearrange("p a b c -> p (a b c)"),
                                        at_hi[:, ko, q * CW:(q + 1) * CW].bitcast(f32), ALU.subtract
                                        ).then_inc(at_ready, 1)
            dve.wait_ge(bo_added, TT // 2)
            for b in range(TT // 2):
                dve.wait_ge(wo_psum, b + 1)
                nc.vector.tensor_tensor(x_tok[:, 2 * b:2 * b + 2, :], x_tok[:, 2 * b:2 * b + 2, :],
                                        ps[:, b, :].rearrange("p (a b) -> p a b", a=2), ALU.add
                                        ).then_inc(ln1_sum, 1)
            for t in range(TT):
                dve.wait_ge(ln1_sum, t // 2 + 1)
                last = nc.vector.bn_stats(stats[:, t, :], x_tok[:, t, :])
            then(last)
            for t in range(TT):
                nc.vector.bn_aggr(mean_var[:, t, :], stats[:, t, :]).then_inc(ln1_var, 1)
            dve.wait_ge(ln1_std, 1)
            then(nc.vector.reciprocal(rstd[:], std[:]))
            for t in range(TT):
                nc.vector.tensor_scalar(x_tok[:, t, :], x_tok[:, t, :], mean_var[:, t, 0:1], rstd[:, t:t + 1],
                                        ALU.subtract, ALU.mult).then_inc(ln1_ready, 1)
            for t in range(KO * CH):
                c, ko = t // KO, t % KO
                dve.wait_ge(yt_hi_ready, t + 1)
                nc.vector.tensor_tensor(yt_lo[:, ko, c * CW:(c + 1) * CW], ps[:, t, :],
                                        yt_hi[:, ko, c * CW:(c + 1) * CW].bitcast(f32), ALU.subtract
                                        ).then_inc(yt_ready, 1)
            dve.sem_inc(gate_up_free, 2)
            dve.sem_inc(down_free, TPC)
            dve.sem_inc(h_ready, 2)

            with dve.Fori(0, CH) as c:
                for m in range(MT + 1):
                    if m < MT:
                        u = c * MT + m
                        dve.wait_ge(silu_done, u + 1)
                        dve.wait_ge(h_ready, u + 1)
                        nc.vector.scalar_tensor_tensor(h32[:, m % 2, :], ps[:, 2 + m % 2, :], sup_c[:, m:m + 1],
                                                       sg[:, m % 2, :], ALU.mult, ALU.mult
                                                       ).then_inc(gate_up_free, 1)
                    if m > 0:
                        dve.wait_ge(h_hi_ready, c * MT + m)
                        nc.vector.tensor_tensor(h_lo[:, m - 1, :], h32[:, (m - 1) % 2, :],
                                                h_hi[:, m - 1, :].bitcast(f32), ALU.subtract).then_inc(h_ready, 1)
                for i in range(TPC):
                    t = c * TPC + i
                    dve.wait_ge(down_psum, t + 1)
                    nc.vector.tensor_tensor(z_tmp[:, i % 2, :], ps[:, 4 + i, 0:HID], sdown_b[:], ALU.mult
                                            ).then_inc(down_free, 1)
                    dve.wait_ge(down_free, t + 1 + TPC)
                    nc.vector.tensor_tensor(r_tmp[:, i, :], z_tmp[:, i % 2, :], x_tok[:, bass.ds(t, 1), :]
                                            .rearrange("p a b -> p (a b)"), ALU.add).then_inc(ln2_sum, 1)
                    dve.wait_ge(ln2_sum, t + 1)
                for i in range(TPC):
                    nc.vector.bn_stats(stats_c[:, i, :], r_tmp[:, i, :]).then_inc(ln2_stats, 1)
                nc.vector.tensor_scalar(x_tok[:, bass.ds(c * TPC, TPC), :], r_tmp[:], 1.0, None, ALU.mult
                                        ).then_inc(ln2_saved, 1)
                dve.wait_ge(ln2_stats, (c + 1) * TPC)
                nc.vector.tensor_scalar(stats[:, bass.ds(c * TPC, TPC), :], stats_c[:], 1.0, None, ALU.mult
                                        ).then_inc(ln2_saved, 1)
                dve.wait_ge(ln2_saved, (c + 1) * 2)
            for t in range(TT):
                nc.vector.bn_aggr(mean_var[:, t, :], stats[:, t, :]).then_inc(ln2_var, 1)
            dve.wait_ge(ln2_std, 1)
            nc.vector.reciprocal(rstd[:], std[:]).then_inc(ln2_rstd, 1)
            dve.wait_ge(ln2_rstd, 1)
            for t in range(TT):
                nc.vector.tensor_scalar(x_tok[:, t, :], x_tok[:, t, :], mean_var[:, t, 0:1], rstd[:, t:t + 1],
                                        ALU.subtract, ALU.mult).then_inc(ln2_ready, 1)

        @block.tensor
        def _(pe):
            pe.wait_ge(consts_ready, 2)
            for c in range(CH):
                pe.wait_ge(x_loaded[c], 16)
                for ko in range(KO):
                    for i in range(TPC):
                        last = nc.tensor.transpose(ps[:, KO * c + ko, i * P:(i + 1) * P],
                                                   x_tok[:, TPC * c + i, ko * P:(ko + 1) * P], ident[:])
                    last.then_inc(xt_psum, 1)

            def products(dst, hi_w, lo_w, hi_x, lo_x):
                for ko in range(KO):
                    for j, (w, x) in enumerate(((hi_w, hi_x), (hi_w, lo_x), (lo_w, hi_x))):
                        last = nc.tensor.matmul(dst, w(ko), x(ko), start=(ko == 0 and j == 0),
                                                stop=(ko == KO - 1 and j == 2))
                return last

            pe.wait_ge(w_ready, 4)
            for n, (c, k) in enumerate(UNITS):
                pe.wait_ge(xt_ready, max(KO * (c + 1), min(n + 1, KO * CH)))
                if n >= 8:
                    if qk_before(n - 7):
                        pe.wait_ge(squares_ready, qk_before(n - 7))
                        pe.wait_ge(rest_ready, qk_before(n - 7))
                    if v_before(n - 7):
                        pe.wait_ge(v_ready, v_before(n - 7))
                if k < 4:
                    i, m = k // 2, k % 2
                    last = products(ps[:, n % 8, :],
                                    lambda ko: w_hi[:, i, ko, m * P:(m + 1) * P],
                                    lambda ko: w_lo[:, i, ko, m * P:(m + 1) * P],
                                    lambda ko: xt_hi[:, ko, c * CW:(c + 1) * CW],
                                    lambda ko: xt_lo[:, ko, c * CW:(c + 1) * CW])
                else:
                    for a in range(2):
                        t = TPC * c + 2 * (k - 4) + a
                        last = products(ps[:, n % 8, a * HID:(a + 1) * HID],
                                        lambda ko: xt_hi[:, ko, t * P:(t + 1) * P],
                                        lambda ko: xt_lo[:, ko, t * P:(t + 1) * P],
                                        lambda ko: w_hi[:, 2, ko, :],
                                        lambda ko: w_lo[:, 2, ko, :])
                last.then_inc(proj_psum, 1)

            pe.wait_ge(squares_ready, len(QK))
            pe.wait_ge(rest_ready, len(QK))
            pe.wait_ge(v_ready, TT // 2)
            for k in range(4):
                for c in range(CH):
                    last = nc.tensor.matmul(ps[32 * c:32 * c + 32, k, :], head_sum[:],
                                            squares[:, k, c * CW:(c + 1) * CW], start=True, stop=True)
            last.then_inc(norms_psum, 1)

            pe.wait_ge(flag_ready, 1)
            need_exact = pe.value_load(exact_flag[0:1, 0:1], min_val=0, max_val=1)
            with pe.If(need_exact > 0):
                with pe.Fori(0, NH) as h:
                    pe.wait_ge(gen_loaded, (h + 1) * STACK)
                    for t in range(TT):
                        pe.wait_ge(gen_max, h * TT + t + 1)
                        for b in range(CH):
                            last = nc.tensor.matmul(ps[:, 4 * (t % 2) + b, :], q_stack[0][0:SROW, t * P:(t + 1) * P],
                                                    k_stack[0][0:SROW, b * CW:(b + 1) * CW], start=True, stop=True)
                        last.then_inc(gen_scores, 1)
                pe.wait_ge(gen_max, NH * TT + 2)
                for a in range(2):
                    nc.tensor.transpose(ps[:, 0, a * P:(a + 1) * P],
                                        row_max[:].rearrange("p h (b a) -> p (h b) a", a=2)[:, :, a], ident[:]
                                        ).then_inc(gen_turned, 1)

            def prob_times_v(slot, n, kt):
                for q in range(CH):
                    last = nc.tensor.matmul(ps[32 * q:32 * q + VW, ACC, :], v_slot[slot][:, kt, :],
                                            probs[:, n % 3, q, :], start=(kt == 0), stop=(kt == TT - 1))
                last.then_inc(pv_done, 1)

            def head(h, j, i):
                slot, first = j % 3, (j == 0)
                for kt in range(TT):
                    u = h * TT + kt
                    n = j * TT + kt
                    if kt == 0:
                        pe.wait_ge(stack_loaded[slot], (i + 1 + j // 3) * (STACK + SHIFT))
                    for half in range(2):
                        ring = (2 * n + half) % 3
                        if not (first and 2 * kt + half < 3):
                            pe.wait_ge(exp_done, 2 * u + half - 2)
                        for q in (2 * half, 2 * half + 1):
                            last = nc.tensor.matmul(ps[:, 2 * ring + q % 2, :],
                                                    k_stack[slot][0:ROWS, kt * P:(kt + 1) * P],
                                                    q_stack[slot][0:ROWS, q * CW:(q + 1) * CW], start=True, stop=True)
                        last.then_inc(scores_ready, 1)
                    if kt >= 2:
                        if kt == 2:
                            pe.wait_ge(v_slot_ready, h + 1)
                            if not first:
                                pe.wait_ge(attn_saved, h)
                        pe.wait_ge(exp_done, 2 * (u - 1))
                        prob_times_v(slot, n - 2, kt - 2)
                    elif not first:
                        pe.wait_ge(exp_done, 2 * (u - 1))
                        prob_times_v((j - 1) % 3, n - 2, TT - 2 + kt)

            pe.wait_ge(shift_ready, 1)
            head(0, 0, 0)
            with pe.Fori(0, (NH - 1) // 3) as i:
                for j in range(1, 4):
                    head(i * 3 + j, j, i)
            for kt in (TT - 2, TT - 1):
                pe.wait_ge(exp_done, 2 * ((NH - 1) * TT + kt + 1))
                prob_times_v(0, 3 * TT + kt, kt)

            pe.wait_ge(attn_saved, NH)
            for g in range(16):
                ug, ko = g // 2, g % 2
                if g >= 6:
                    pe.wait_ge(attn_scaled, g - 5)
                for k in range(4):
                    last = nc.tensor.transpose(
                        ps[:, g % 6, k * P:(k + 1) * P],
                        attn[:, 4 * ug + k, HPB * ko:HPB * (ko + 1), :].rearrange("p r h -> p (r h)"), ident[:])
                last.then_inc(attn_turned, 1)
            pe.wait_ge(at_ready, 8)
            for t in range(TT):
                last = products(ps[:, t // 2, (t % 2) * HID:(t % 2 + 1) * HID],
                                lambda ko: at_hi[:, ko, t * P:(t + 1) * P], lambda ko: at_lo[:, ko, t * P:(t + 1) * P],
                                lambda ko: wo_hi[:, ko, :], lambda ko: wo_lo[:, ko, :])
                if t % 2:
                    last.then_inc(wo_psum, 1)
            for c in range(CH):
                pe.wait_ge(ln1_ready, TPC * (c + 1))
                for ko in range(KO):
                    for i in range(TPC):
                        last = nc.tensor.transpose(ps[:, KO * c + ko, i * P:(i + 1) * P],
                                                   x_tok[:, TPC * c + i, ko * P:(ko + 1) * P], ident[:])
                    last.then_inc(yt_psum, 1)
            pe.wait_ge(yt_ready, KO * CH)
            pe.wait_ge(ffn_w_ready, 3)

            def down(m):
                for i in range(TPC):
                    for j, h in enumerate((h_hi, h_lo)):
                        last = nc.tensor.matmul(ps[:, 4 + i, 0:HID], h[:, m, i * P:(i + 1) * P], wd[:, m, :],
                                                start=(m == 0 and j == 0), stop=(m == MT - 1 and j == 1))
                    if m == MT - 1:
                        last.then_inc(down_psum, 1)

            with pe.Fori(0, CH) as c:
                for m in range(MT + 2):
                    if m < MT:
                        pe.wait_ge(gate_up_free, c * MT + m + 1)
                        for w, bank in ((wg, m % 2), (wu, 2 + m % 2)):
                            for ko in range(KO):
                                for j, y in enumerate((yt_hi, yt_lo)):
                                    last = nc.tensor.matmul(ps[:, bank, :], w[:, ko, m * P:(m + 1) * P],
                                                            y[:, ko, bass.ds(c * CW, CW)],
                                                            start=(ko == 0 and j == 0), stop=(ko == KO - 1 and j == 1))
                        last.then_inc(gate_up_psum, 1)
                    if m >= 2:
                        pe.wait_ge(h_ready, c * MT + m + 1)
                        if m == 2:
                            pe.wait_ge(down_free, (c + 1) * TPC)
                        down(m - 2)


_INS = ['L0_attn_X', 'L0_attn_Wq', 'L0_attn_bq', 'L0_attn_Wk', 'L0_attn_bk', 'L0_attn_Wv', 'L0_attn_bv', 'L0_attn_Wo',
        'L0_attn_bo', 'L0_ffn_w_gate', 'L0_ffn_w_up', 'L0_ffn_w_down', 'L0_ffn_s_gate', 'L0_ffn_s_up', 'L0_ffn_s_down']


def kernel(**inputs):
    import concourse.bacc as _bacc
    from concourse.bass_utils import run_bass_kernel_spmd as _run

    nc = _bacc.Bacc("TRN2", target_bir_lowering=False, num_devices=1)
    arrays, args = {}, []
    for name in _INS:
        a = np.ascontiguousarray(inputs[name])
        if a.dtype == np.int8:
            a = a.view(np.int32)
        arrays[f"in_{name}"] = a
        args.append(nc.dram_tensor(f"in_{name}", a.shape, mybir.dt.from_np(a.dtype), kind="ExternalInput").ap())
    shape = np.shape(inputs['L0_attn_X'])
    args.append(nc.dram_tensor("out_0", shape, mybir.dt.float32, kind="ExternalOutput").ap())
    layer_program(nc, *args)
    r = _run(nc, [arrays], core_ids=[0])
    return r.results[0]["out_0"]
```

```python
import numpy as np
import concourse.bass as bass
from concourse import mybir
from contextlib import ExitStack


def layer_program(nc, X, Wq, bq, Wk, bk, Wv, bv, Wo, bo, w_gate, w_up, w_down, s_gate, s_up, s_down, out):
    f32, f32r, bf16 = mybir.dt.float32, mybir.dt.float32r, mybir.dt.bfloat16
    i8, i32 = mybir.dt.int8, mybir.dt.int32
    ALU = mybir.AluOpType
    ACT = mybir.ActivationFunctionType
    AXX = mybir.AxisListType.X
    MAX_ACROSS = bass.bass_isa.ReduceOp.max

    P = 128
    S, HID = X.shape[1], X.shape[2]
    NH = 16
    HD = HID // NH
    INTER = s_gate.shape[0]
    KO = HID // P
    TT = S // P
    CW = 512
    CH = S // CW
    TPC = TT // CH
    MT = INTER // P
    HPB = P // HD
    NPROD = 6
    SROW = NPROD * HD
    ROWS = SROW + 3
    PRODUCTS = [(3, 0, 0), (2, 1, 0), (1, 2, 0)]
    VW = 32
    NSLOT = 3
    SCALE = float(HD) ** -0.5
    SAFE = 40.0
    EPS = 1e-5

    with ExitStack() as ctx:
        arena_at = (nc.sbuf_base + 63) // 64 * 64
        place_at = [arena_at]

        def place(name, shape, dt, at=None):
            size = int(np.prod(shape[1:])) * {f32: 4, f32r: 4, i32: 4, bf16: 2, i8: 1}[dt]
            where = place_at[0] if at is None else at
            if at is None:
                place_at[0] += (size + 63) // 64 * 64
            return nc.alloc_sbuf_tensor_at(name, shape, dt, offset=where)

        def region(size):
            at = place_at[0]
            place_at[0] += size
            return at

        KB = 1024
        x_tok = place("x_tok", [P, TT, HID], f32)
        gate8 = place("gate8", [P, KO, INTER // 4], i32)
        up8 = place("up8", [P, KO, INTER // 4], i32)
        down8 = place("down8", [P, MT, HID // 4], i32)
        wo = place("wo", [P, KO, HID], f32)
        ident = place("ident", [P, P], f32)
        head_sum = place("head_sum", [P, 32], bf16)
        bq_c = place("bq_c", [P, KO], f32)
        bk_c = place("bk_c", [P, KO], f32)
        bv_b = place("bv_b", [P, 2, HID], f32)
        bo_b = place("bo_b", [P, 2, HID], f32)
        sdown_b = place("sdown_b", [P, HID], f32)
        sgate_c = place("sgate_c", [P, MT], f32)
        sup_c = place("sup_c", [P, MT], f32)
        norm_max = place("norm_max", [P, 4], f32)
        norm_qk = place("norm_qk", [P, 2], f32)
        norm_all = place("norm_all", [P, 2], f32)
        norm_sum = place("norm_sum", [P, 1], f32)
        shift_neg = place("shift_neg", [P, 1], f32)
        exact_flag = place("exact_flag", [P, 1], i32)
        row_max = place("row_max", [P, NH, TT], f32)
        shift = place("shift", [P, 3, 2 * P], bf16)
        shift_rest = place("shift_rest", [P, 2 * P], f32)
        den = place("den", [P, 2, 8, 4], f32)
        stats = place("stats", [P, TT, 6], f32)
        mean_var = place("mean_var", [P, TT, 2], f32)
        var_eps = place("var_eps", [P, TPC], f32)
        rstd = place("rstd", [P, TT], f32)
        minus_half = place("minus_half", [P, TPC], f32)
        q_stack = [place(f"q_stack{i}", [ROWS, S], bf16) for i in range(NSLOT)]
        k_stack = [place(f"k_stack{i}", [ROWS, S], bf16) for i in range(NSLOT)]
        v_slot = [place(f"v_slot{i}", [P, TT, VW], f32) for i in range(NSLOT)]

        at = region(16 * KB)
        v_all = place("v_all", [P, TT, HID], f32, at)
        wd = place("wd", [P, MT, HID], f32r, at)
        h32 = place("h32", [P, 2, CW], f32, at + 8 * KB)
        sg = place("sg", [P, 2, CW], f32, at + 12 * KB)
        at = region(40 * KB)
        w_raw = place("w_raw", [P, 3, KO * HID], f32, at)
        w_hi = place("w_hi", [P, 3, KO, HID], f32r, at + 8 * KB)
        w_lo = place("w_lo", [P, 3, KO, HID], f32r, at + 14 * KB)
        rest = place("rest", [P, 2, CW], f32, at + 20 * KB)
        squares = place("squares", [P, 4, S], bf16, at + 24 * KB)
        attn = place("attn", [P, S // NH // 4, NH, NH], f32, at)
        h_hi = place("h_hi", [P, MT, CW], f32r, at)
        h_lo = place("h_lo", [P, MT, CW], f32r, at + 16 * KB)
        z_tmp = place("z_tmp", [P, 2, HID], f32, at + 32 * KB)
        r_tmp = place("r_tmp", [P, TPC, HID], f32, at + 34 * KB)
        at = region(48 * KB)
        q_parts = place("q_parts", [P, KO, 3, S], bf16, at)
        k_parts = place("k_parts", [P, KO, 3, S], bf16, at + 24 * KB)
        at32 = place("at32", [P, KO, HD, 4, 32], f32, at)
        out_tmp = place("out_tmp", [P, 2, TPC, HID], f32, at + 16 * KB)
        wg = place("wg", [P, KO, INTER], f32r, at + 32 * KB)
        wu = place("wu", [P, KO, INTER], f32r, at + 40 * KB)
        at = region(32 * KB)
        xt_hi = place("xt_hi", [P, KO, S], f32r, at)
        xt_lo = place("xt_lo", [P, KO, S], f32r, at + 16 * KB)
        probs = place("probs", [P, 3, CH, CW], f32, at)
        yt_hi = place("yt_hi", [P, KO, S], f32r, at)
        yt_lo = place("yt_lo", [P, KO, S], f32r, at + 16 * KB)

        ps = ctx.enter_context(nc.psum_tensor("ps", [P, 8, CW], f32))
        ACC = 6

        def sem(name):
            return ctx.enter_context(nc.semaphore(name))

        x_loaded = [sem(f"x_loaded{c}") for c in range(CH)]
        w_loaded = [sem(f"w_loaded{i}") for i in range(4)]
        bias_loaded = sem("bias_loaded")
        late_loaded = sem("late_loaded")
        consts_ready = sem("consts_ready")
        pool_step = sem("pool_step")
        dve_step = sem("dve_step")
        pad_ready = sem("pad_ready")
        w_hi_ready = sem("w_hi_ready")
        w_ready = sem("w_ready")
        xt_psum = sem("xt_psum")
        xt_hi_ready = sem("xt_hi_ready")
        xt_ready = sem("xt_ready")
        proj_psum = sem("proj_psum")
        part1_ready = sem("part1_ready")
        squares_ready = sem("squares_ready")
        rest_ready = sem("rest_ready")
        part2_ready = sem("part2_ready")
        part3_ready = sem("part3_ready")
        v_ready = sem("v_ready")
        norms_psum = sem("norms_psum")
        norms_ready = sem("norms_ready")
        norms_reduced = sem("norms_reduced")
        flag_ready = sem("flag_ready")
        gen_loaded = sem("gen_loaded")
        gen_scores = sem("gen_scores")
        gen_max = sem("gen_max")
        gen_turned = sem("gen_turned")
        gen_split = sem("gen_split")
        gen_reloaded = sem("gen_reloaded")
        shift_ready = sem("shift_ready")
        stack_loaded = [sem(f"stack_loaded{i}") for i in range(NSLOT)]
        v_slot_ready = sem("v_slot_ready")
        scores_ready = sem("scores_ready")
        exp_done = sem("exp_done")
        pv_done = sem("pv_done")
        attn_saved = sem("attn_saved")
        ffn_w_ready = sem("ffn_w_ready")
        bo_added = sem("bo_added")
        attn_turned = sem("attn_turned")
        attn_scaled = sem("attn_scaled")
        wo_psum = sem("wo_psum")
        ln1_sum = sem("ln1_sum")
        ln1_var = sem("ln1_var")
        ln1_rstd = sem("ln1_rstd")
        ln1_ready = sem("ln1_ready")
        yt_psum = sem("yt_psum")
        yt_hi_ready = sem("yt_hi_ready")
        yt_ready = sem("yt_ready")
        gate_up_psum = sem("gate_up_psum")
        gate_up_free = sem("gate_up_free")
        silu_done = sem("silu_done")
        h_hi_ready = sem("h_hi_ready")
        h_ready = sem("h_ready")
        down_psum = sem("down_psum")
        down_free = sem("down_free")
        ln2_sum = sem("ln2_sum")
        ln2_stat = sem("ln2_stat")
        ln2_gate = sem("ln2_gate")
        ln2_aggr = sem("ln2_aggr")
        ln2_var = sem("ln2_var")
        ln2_rstd = sem("ln2_rstd")
        ln2_ready = sem("ln2_ready")
        stored = [sem(f"stored{i}") for i in range(2)]

        block = ctx.enter_context(nc.Block())

        x_view = X.rearrange("a (t p) n -> p (a t) n", p=P)
        out_view = out.rearrange("a (t p) n -> p (a t) n", p=P)
        STACK = 16 * 2 * len(PRODUCTS)
        SHIFT = 16 * 3

        QK = [(c, k) for c in range(CH) for k in (0, 2, 1, 3)]
        VP = list(range(TT // 2))
        V_BANK = 4

        @block.sync
        def _(sp):
            for c in range(CH):
                sp.dma_start(x_tok[:, TPC * c:TPC * (c + 1), :], x_view[:, TPC * c:TPC * (c + 1), :]
                             ).then_inc(x_loaded[c], 16)
            sp.dma_start(gate8[:], w_gate.rearrange("(k p) n -> p k n", p=P)).then_inc(late_loaded, 16)
            sp.dma_start(up8[:], w_up.rearrange("(k p) n -> p k n", p=P)).then_inc(late_loaded, 16)
            sp.dma_start(down8[:], w_down.rearrange("(k p) n -> p k n", p=P)).then_inc(late_loaded, 16)

            def load_stack(h, slot, done):
                blk, row = h // HPB, HD * (h % HPB)
                at = 0
                for n, q_part, k_part in PRODUCTS:
                    sp.dma_start(k_stack[slot][at:at + n * HD, :],
                                 k_parts[row:row + HD, blk, k_part:k_part + n, :]).then_inc(done, 16)
                    sp.dma_start(q_stack[slot][at:at + n * HD, :],
                                 q_parts[row:row + HD, blk, q_part:q_part + 1, :].to_broadcast([HD, n, S])
                                 ).then_inc(done, 16)
                    at += n * HD

            def load_shift(h, slot):
                for i in range(3):
                    sp.dma_start(q_stack[slot][SROW + i:SROW + i + 1, :],
                                 shift[h * HPB:(h + 1) * HPB, i, :]).then_inc(stack_loaded[slot], 16)

            def refill(h, slot):
                sp.wait_ge(scores_ready, (h - NSLOT + 1) * 2 * TT)
                load_stack(h, slot, stack_loaded[slot])
                load_shift(h, slot)

            sp.wait_ge(part1_ready, len(QK) - 2)
            sp.wait_ge(part2_ready, len(QK) - 2)
            sp.wait_ge(part3_ready, len(QK) - 2)
            load_stack(0, 0, stack_loaded[0])
            sp.wait_ge(flag_ready, 1)
            sp.wait_ge(part3_ready, len(QK))
            need_exact = sp.value_load(exact_flag[0:1, 0:1], min_val=0, max_val=1)
            with sp.If(need_exact > 0):
                sp.wait_ge(stack_loaded[0], STACK)
                for h in range(NH):
                    if h:
                        sp.wait_ge(gen_max, h * TT + 2)
                    load_stack(h, 0, gen_loaded)
                sp.wait_ge(gen_max, NH * TT + 2)
                load_stack(0, 0, gen_reloaded)
                sp.wait_ge(gen_reloaded, STACK)
            sp.wait_ge(shift_ready, 1)
            load_shift(0, 0)
            for h in range(1, NSLOT):
                load_stack(h, h, stack_loaded[h])
                load_shift(h, h)
            for h in range(NSLOT, NH):
                refill(h, h % NSLOT)
            with sp.Fori(0, CH // 2) as i:
                for b in range(2):
                    c = i * 2 + b
                    sp.wait_ge(ln2_ready, (c + 1) * TPC)
                    sp.dma_start(out_view[:, bass.ds(c * TPC, TPC), :], out_tmp[:, b, :, :]).then_inc(stored[b], 16)
            for b in range(2):
                sp.wait_ge(stored[b], 16 * CH // 2)

        @block.gpsimd
        def _(pool):
            steps = [0]

            def then(instruction):
                steps[0] += 1
                instruction.then_inc(pool_step, 1)
                pool.wait_ge(pool_step, steps[0])

            then(nc.gpsimd.memset(ident[:], 0.0))
            nc.gpsimd.affine_select(out=ident[:], in_=ident[:], compare_op=ALU.not_equal, fill=1.0, base=0,
                                    pattern=[[-1, P]], channel_multiplier=1).then_inc(consts_ready, 1)
            then(nc.gpsimd.memset(head_sum[:], 1.0))
            then(nc.gpsimd.affine_select(out=head_sum[:], in_=head_sum[:], compare_op=ALU.is_ge, fill=0.0, base=0,
                                         pattern=[[-HD, 32]], channel_multiplier=1))
            nc.gpsimd.affine_select(out=head_sum[:], in_=head_sum[:], compare_op=ALU.is_ge, fill=0.0, base=HD - 1,
                                    pattern=[[HD, 32]], channel_multiplier=-1).then_inc(consts_ready, 1)
            nc.gpsimd.memset(minus_half[:], -0.5).then_inc(pad_ready, 1)
            for s in range(NSLOT):
                then(nc.gpsimd.memset(v_slot[s][:], 0.0))
                nc.gpsimd.memset(v_slot[s][:, :, HD:HD + 1], 1.0).then_inc(pad_ready, 1)
            for n, (c, k) in enumerate(QK):
                parts = q_parts if k < 2 else k_parts
                pool.wait_ge(rest_ready, n + 1)
                nc.gpsimd.tensor_copy(parts[:, k % 2, 1, c * CW:(c + 1) * CW], rest[:, n % 2, :]
                                      ).then_inc(part2_ready, 1)
            pool.wait_ge(norms_ready, 1)
            nc.gpsimd.partition_all_reduce(norm_all[:], norm_qk[:], P, MAX_ACROSS).then_inc(norms_reduced, 1)
            pool.wait_ge(bias_loaded, 16 * 9)
            pool.wait_ge(xt_ready, 2 * CH)
            for t in range(0, TT, 2):
                nc.gpsimd.tensor_tensor(x_tok[:, t:t + 2, :], x_tok[:, t:t + 2, :], bo_b[:], ALU.add
                                        ).then_inc(bo_added, 1)
            pool.wait_ge(late_loaded, 16 * 3)
            pool.wait_ge(scores_ready, NH * 2 * TT)
            nc.gpsimd.tensor_copy(wg[:], gate8[:].bitcast(i8)).then_inc(ffn_w_ready, 1)
            nc.gpsimd.tensor_copy(wu[:], up8[:].bitcast(i8)).then_inc(ffn_w_ready, 1)
            pool.wait_ge(v_slot_ready, NH)
            nc.gpsimd.tensor_copy(wd[:], down8[:].bitcast(i8)).then_inc(ffn_w_ready, 1)
            pool.wait_ge(pad_ready, 2 * NSLOT + 1)
            for c in range(CH):
                pool.wait_ge(ln1_var, c + 1)
                nc.gpsimd.tensor_tensor(rstd[:, TPC * c:TPC * (c + 1)], var_eps[:], minus_half[:], ALU.pow
                                        ).then_inc(ln1_rstd, 1)
            with pool.Fori(0, CH) as c:
                pool.wait_ge(ln2_var, c + 1)
                nc.gpsimd.tensor_tensor(rstd[:, 0:TPC], var_eps[:], minus_half[:], ALU.pow).then_inc(ln2_rstd, 1)

        def three_heads(engine, head):
            head(0, 0)
            with engine.Fori(0, (NH - 1) // 3) as i:
                for j in range(1, 4):
                    head(i * 3 + j, j)

        @block.scalar
        def _(act):
            for i, w in enumerate((Wq, Wk, Wv)):
                act.dma_start(w_raw[:, i, :].rearrange("p (k n) -> p k n", k=KO),
                              w.rearrange("(k p) n -> p k n", p=P)).then_inc(w_loaded[i], 16)
            act.dma_start(wo[:], Wo.rearrange("(k p) n -> p k n", p=P)).then_inc(w_loaded[3], 16)
            act.dma_start(bq_c[:], bq.rearrange("(k p) -> p k", p=P),
                          allow_slow_non_contiguous=True).then_inc(bias_loaded, 16)
            act.dma_start(bk_c[:], bk.rearrange("(k p) -> p k", p=P),
                          allow_slow_non_contiguous=True).then_inc(bias_loaded, 16)
            for i in range(2):
                act.dma_start(bv_b[:, i, :], bv.partition_broadcast(P)).then_inc(bias_loaded, 16)
                act.dma_start(bo_b[:, i, :], bo.partition_broadcast(P)).then_inc(bias_loaded, 16)
            act.dma_start(sdown_b[:], s_down.partition_broadcast(P)).then_inc(bias_loaded, 16)
            act.dma_start(sgate_c[:], s_gate.rearrange("(k p) -> p k", p=P),
                          allow_slow_non_contiguous=True).then_inc(bias_loaded, 16)
            act.dma_start(sup_c[:], s_up.rearrange("(k p) -> p k", p=P),
                          allow_slow_non_contiguous=True).then_inc(bias_loaded, 16)
            for i in range(3):
                act.wait_ge(w_loaded[i], 16)
                nc.scalar.copy(w_hi[:, i, :, :], w_raw[:, i, :].rearrange("p (k n) -> p k n", k=KO)
                               ).then_inc(w_hi_ready, 1)
            for t in range(KO * CH):
                c, ko = t // KO, t % KO
                act.wait_ge(xt_psum, t + 1)
                nc.scalar.copy(xt_hi[:, ko, c * CW:(c + 1) * CW], ps[:, t, :]).then_inc(xt_hi_ready, 1)
            act.wait_ge(bias_loaded, 16 * 9)
            for n, (c, k) in enumerate(QK):
                parts, b_c = (q_parts, bq_c) if k < 2 else (k_parts, bk_c)
                act.wait_ge(proj_psum, n + 1)
                nc.scalar.activation(parts[:, k % 2, 0, c * CW:(c + 1) * CW], ps[:, n % 8, :], ACT.Identity,
                                     bias=b_c[:, k % 2:k % 2 + 1]).then_inc(part1_ready, 1)
                nc.scalar.activation(squares[:, k, c * CW:(c + 1) * CW], ps[:, n % 8, :], ACT.Square,
                                     bias=b_c[:, k % 2:k % 2 + 1]).then_inc(squares_ready, 1)

            def head(h, j):
                for kt in range(TT):
                    u = h * TT + kt
                    for half in range(2):
                        ring = (2 * (j * TT + kt) + half) % 3
                        act.wait_ge(scores_ready, 2 * u + half + 1)
                        if half == 0 and not (j == 0 and kt < 3):
                            act.wait_ge(pv_done, u - 2)
                        nc.scalar.activation(
                            probs[:, (j * TT + kt) % 3, 2 * half:2 * half + 2, :].rearrange("p a b -> p (a b)"),
                            ps[:, 2 * ring:2 * ring + 2, :].rearrange("p a b -> p (a b)"),
                            ACT.Exp, bias=0.0, scale=SCALE).then_inc(exp_done, 1)

            act.wait_ge(xt_ready, 2 * CH)
            three_heads(act, head)

            for t in range(KO * CH):
                c, ko = t // KO, t % KO
                act.wait_ge(yt_psum, t + 1)
                nc.scalar.copy(yt_hi[:, ko, c * CW:(c + 1) * CW], ps[:, t, :]).then_inc(yt_hi_ready, 1)
            with act.Fori(0, CH) as c:
                for m in range(MT + 1):
                    if m < MT:
                        u = c * MT + m
                        act.wait_ge(gate_up_psum, u + 1)
                        act.wait_ge(gate_up_free, u + 1)
                        nc.scalar.activation(sg[:, m % 2, :], ps[:, m % 2, :], ACT.Silu,
                                             scale=sgate_c[:, m:m + 1]).then_inc(silu_done, 1)
                    if m > 0:
                        act.wait_ge(gate_up_free, c * MT + m + 2)
                        nc.scalar.copy(h_hi[:, m - 1, :], h32[:, (m - 1) % 2, :]).then_inc(h_hi_ready, 1)

        @block.vector
        def _(dve):
            steps = [0]

            def then(instruction):
                steps[0] += 1
                instruction.then_inc(dve_step, 1)
                dve.wait_ge(dve_step, steps[0])

            then(nc.vector.memset(shift[:], 0.0))
            for s in range(NSLOT):
                nc.vector.memset(k_stack[s][SROW:ROWS, :], 1.0).then_inc(pad_ready, 1)
            for i in range(3):
                dve.wait_ge(w_hi_ready, i + 1)
                nc.vector.tensor_tensor(w_lo[:, i, :, :], w_raw[:, i, :].rearrange("p (k n) -> p k n", k=KO),
                                        w_hi[:, i, :, :].bitcast(f32), ALU.subtract).then_inc(w_ready, 1)
            for t in range(KO * CH):
                c, ko = t // KO, t % KO
                dve.wait_ge(xt_hi_ready, t + 1)
                nc.vector.tensor_tensor(xt_lo[:, ko, c * CW:(c + 1) * CW], ps[:, t, :],
                                        xt_hi[:, ko, c * CW:(c + 1) * CW].bitcast(f32), ALU.subtract
                                        ).then_inc(xt_ready, 1)
            dve.wait_ge(bias_loaded, 16 * 9)

            def third_part(n):
                c, k = QK[n]
                parts = q_parts if k < 2 else k_parts
                dve.wait_ge(part2_ready, n + 1)
                nc.vector.tensor_tensor(parts[:, k % 2, 2, c * CW:(c + 1) * CW], rest[:, n % 2, :],
                                        parts[:, k % 2, 1, c * CW:(c + 1) * CW], ALU.subtract
                                        ).then_inc(part3_ready, 1)

            for n, (c, k) in enumerate(QK):
                parts, b_c = (q_parts, bq_c) if k < 2 else (k_parts, bk_c)
                dve.wait_ge(squares_ready, n + 1)
                if n >= 2:
                    dve.wait_ge(part3_ready, n - 1)
                nc.vector.scalar_tensor_tensor(rest[:, n % 2, :], ps[:, n % 8, :], b_c[:, k % 2:k % 2 + 1],
                                               parts[:, k % 2, 0, c * CW:(c + 1) * CW], ALU.add, ALU.subtract
                                               ).then_inc(rest_ready, 1)
                if n >= 1:
                    third_part(n - 1)
            third_part(len(QK) - 1)

            def save_v(n):
                dve.wait_ge(proj_psum, len(QK) + n + 1)
                nc.vector.tensor_tensor(v_all[:, 2 * n:2 * n + 2, :],
                                        ps[:, V_BANK + n % 4, :].rearrange("p (a b) -> p a b", a=2),
                                        bv_b[:], ALU.add).then_inc(v_ready, 1)

            def fill_v_slot(h, slot):
                nc.vector.tensor_scalar(v_slot[slot][:, :, 0:HD], v_all[:, :, bass.ds(h * HD, HD)], 1.0, None,
                                        ALU.mult).then_inc(v_slot_ready, 1)

            save_v(0)
            save_v(1)
            dve.wait_ge(norms_psum, 1)
            then(nc.vector.reduce_max(norm_max[:], ps[:, 0:4, :], AXX))
            nc.vector.tensor_tensor(norm_qk[:], norm_max[:, 0:4:2], norm_max[:, 1:4:2], ALU.max
                                    ).then_inc(norms_ready, 1)
            for n in VP[2:5]:
                save_v(n)
            dve.wait_ge(norms_reduced, 1)
            then(nc.vector.tensor_tensor(norm_sum[:], norm_all[:, 0:1], norm_all[:, 1:2], ALU.add))
            then(nc.vector.tensor_scalar(shift_neg[:], norm_sum[:], -0.51, None, ALU.mult))
            then(nc.vector.tensor_scalar(shift[:, 0, :], shift[:, 1, :], shift_neg[:, 0:1], None, ALU.add))
            then(nc.vector.tensor_scalar(norm_sum[:], norm_sum[:], 0.51 * SCALE, SAFE, ALU.mult, ALU.is_le))
            nc.vector.tensor_scalar(exact_flag[:], norm_sum[:], -1.0, 1.0, ALU.mult, ALU.add).then_inc(flag_ready, 1)
            dve.wait_ge(flag_ready, 1)
            for n in VP[5:]:
                save_v(n)
            dve.wait_ge(pad_ready, 2 * NSLOT + 1)
            dve.wait_ge(v_ready, TT // 2)
            for h in range(NSLOT):
                fill_v_slot(h, h)
            need_exact = dve.value_load(exact_flag[0:1, 0:1], min_val=0, max_val=1)
            with dve.If(need_exact > 0):
                dve.sem_inc(gen_max, 2)
                with dve.Fori(0, NH) as h:
                    for t in range(TT):
                        dve.wait_ge(gen_scores, h * TT + t + 1)
                        nc.vector.reduce_max(row_max[:, bass.ds(h, 1), t], ps[:, 4 * (t % 2):4 * (t % 2) + 4, :]
                                             .rearrange("p a b -> p (a b)"), AXX).then_inc(gen_max, 1)
                dve.wait_ge(gen_turned, 2)
                turned = ps[:, 0, 0:2 * P]
                nc.vector.tensor_scalar(shift[:, 0, :], turned, -1.0, None, ALU.mult).then_inc(gen_split, 1)
                dve.wait_ge(gen_split, 1)
                nc.vector.scalar_tensor_tensor(shift_rest[:], turned, -1.0, shift[:, 0, :], ALU.mult, ALU.subtract
                                               ).then_inc(gen_split, 1)
                dve.wait_ge(gen_split, 2)
                nc.vector.tensor_copy(shift[:, 1, :], shift_rest[:]).then_inc(gen_split, 1)
                dve.wait_ge(gen_split, 3)
                nc.vector.tensor_tensor(shift[:, 2, :], shift_rest[:], shift[:, 1, :], ALU.subtract
                                        ).then_inc(gen_split, 1)
                dve.wait_ge(gen_split, 4)
            dve.sem_inc(shift_ready, 1)

            def head(h, j):
                dve.wait_ge(pv_done, (h + 1) * TT)
                nc.vector.tensor_scalar(attn[:, :, :, bass.ds(h, 1)],
                                        ps[:, ACC, :].rearrange("p (u r o) -> p u r o", r=NH, o=1), 1.0, None,
                                        ALU.mult).then_inc(attn_saved, 1)

            def head_and_fill(h, j):
                head(h, j)
                fill_v_slot(h + NSLOT, j % 3)

            head_and_fill(0, 0)
            with dve.Fori(0, (NH - 1) // 3 - 1) as i:
                for j in range(1, 4):
                    head_and_fill(i * 3 + j, j)
            for h in range(NH - NSLOT, NH):
                head(h, h)

            for g in range(8):
                ko, ug, b = g % 2, g // 2, 2 * (g % 3)
                turned = ps[:, b:b + 2, :].rearrange("p b (u j d) -> p (b u) j d", u=4, d=32)
                dve.wait_ge(attn_turned, g + 1)
                then(nc.vector.reciprocal(den[:, g % 2, :, :], turned[:, :, :, HD]))
                nc.vector.tensor_tensor(
                    at32[:, ko, :, :, 8 * ug:8 * ug + 8].rearrange("p d j u -> p u j d"), turned[:, :, :, 0:HD],
                    den[:, g % 2, :, :].unsqueeze(3).to_broadcast([P, 8, 4, HD]), ALU.mult).then_inc(attn_scaled, 1)
            dve.wait_ge(bo_added, TT // 2)

            def ln1_stats(c):
                for b in (2 * c, 2 * c + 1):
                    dve.wait_ge(wo_psum, b + 1)
                    nc.vector.tensor_tensor(x_tok[:, 2 * b:2 * b + 2, :], x_tok[:, 2 * b:2 * b + 2, :],
                                            ps[:, b, :].rearrange("p (a b) -> p a b", a=2), ALU.add
                                            ).then_inc(ln1_sum, 1)
                for t in range(TPC * c, TPC * (c + 1)):
                    dve.wait_ge(ln1_sum, t // 2 + 1)
                    last = nc.vector.bn_stats(stats[:, t, :], x_tok[:, t, :])
                then(last)
                for t in range(TPC * c, TPC * (c + 1)):
                    last = nc.vector.bn_aggr(mean_var[:, t, :], stats[:, t, :])
                then(last)
                if c:
                    dve.wait_ge(ln1_rstd, c)
                nc.vector.tensor_scalar(var_eps[:], mean_var[:, TPC * c:TPC * (c + 1), 1], EPS, None, ALU.add
                                        ).then_inc(ln1_var, 1)

            def ln1_scale(c):
                dve.wait_ge(ln1_rstd, c + 1)
                for t in range(TPC * c, TPC * (c + 1)):
                    nc.vector.tensor_scalar(x_tok[:, t, :], x_tok[:, t, :], mean_var[:, t, 0:1], rstd[:, t:t + 1],
                                            ALU.subtract, ALU.mult).then_inc(ln1_ready, 1)

            def ln1_lo(c):
                for ko in range(KO):
                    t = KO * c + ko
                    dve.wait_ge(yt_hi_ready, t + 1)
                    nc.vector.tensor_tensor(yt_lo[:, ko, c * CW:(c + 1) * CW], ps[:, t, :],
                                            yt_hi[:, ko, c * CW:(c + 1) * CW].bitcast(f32), ALU.subtract
                                            ).then_inc(yt_ready, 1)

            for c in range(CH + 2):
                if c < CH:
                    ln1_stats(c)
                if 0 <= c - 1 < CH:
                    ln1_scale(c - 1)
                if 0 <= c - 2 < CH:
                    ln1_lo(c - 2)

            dve.sem_inc(gate_up_free, 2)
            dve.sem_inc(down_free, TPC)
            dve.sem_inc(h_ready, 2)

            def ln2_stats(c):
                for i in range(TPC):
                    t = c * TPC + i
                    dve.wait_ge(down_psum, t + 1)
                    nc.vector.tensor_tensor(r_tmp[:, i, :], ps[:, 4 + i, 0:HID], sdown_b[:], ALU.mult
                                            ).then_inc(down_free, 1)
                dve.wait_ge(down_free, (c + 2) * TPC)
                nc.vector.tensor_tensor(r_tmp[:], r_tmp[:], x_tok[:, bass.ds(c * TPC, TPC), :], ALU.add
                                        ).then_inc(ln2_sum, 1)
                dve.wait_ge(ln2_sum, c + 1)
                for i in range(TPC):
                    last = nc.vector.bn_stats(stats[:, i, :], r_tmp[:, i, :])
                last.then_inc(ln2_stat, 1)
                dve.wait_ge(ln2_stat, c + 1)
                dve.sem_inc(ln2_gate, 1)
                for i in range(TPC):
                    last = nc.vector.bn_aggr(mean_var[:, i, :], stats[:, i, :])
                last.then_inc(ln2_aggr, 1)
                dve.wait_ge(ln2_aggr, c + 1)
                nc.vector.tensor_scalar(var_eps[:], mean_var[:, 0:TPC, 1], EPS, None, ALU.add).then_inc(ln2_var, 1)

            def ln2_scale(c, b, first):
                dve.wait_ge(ln2_rstd, c + 1)
                if not first:
                    dve.wait_ge(stored[b], 16)
                for i in range(TPC):
                    nc.vector.tensor_scalar(out_tmp[:, b, i, :], r_tmp[:, i, :], mean_var[:, i, 0:1],
                                            rstd[:, i:i + 1], ALU.subtract, ALU.mult).then_inc(ln2_ready, 1)

            def ffn_chunk(c, b, first):
                for m in range(MT + 1):
                    if m < MT:
                        u = c * MT + m
                        dve.wait_ge(silu_done, u + 1)
                        dve.wait_ge(h_ready, u + 1)
                        nc.vector.scalar_tensor_tensor(h32[:, m % 2, :], ps[:, 2 + m % 2, :], sup_c[:, m:m + 1],
                                                       sg[:, m % 2, :], ALU.mult, ALU.mult
                                                       ).then_inc(gate_up_free, 1)
                    if m > 0:
                        dve.wait_ge(h_hi_ready, c * MT + m)
                        nc.vector.tensor_tensor(h_lo[:, m - 1, :], h32[:, (m - 1) % 2, :],
                                                h_hi[:, m - 1, :].bitcast(f32), ALU.subtract).then_inc(h_ready, 1)
                    if m == 2 and not first:
                        ln2_stats(c - 1)
                    if m == 4 and not first:
                        ln2_scale(c - 1, 1 - b, isinstance(c, int) and c < 3)

            ffn_chunk(0, 0, True)
            ffn_chunk(1, 1, False)
            ffn_chunk(2, 0, False)
            ffn_chunk(3, 1, False)
            ln2_stats(CH - 1)
            ln2_scale(CH - 1, 1, False)

        @block.tensor
        def _(pe):
            pe.wait_ge(consts_ready, 2)
            for c in range(CH):
                pe.wait_ge(x_loaded[c], 16)
                for ko in range(KO):
                    for i in range(TPC):
                        last = nc.tensor.transpose(ps[:, KO * c + ko, i * P:(i + 1) * P],
                                                   x_tok[:, TPC * c + i, ko * P:(ko + 1) * P], ident[:])
                    last.then_inc(xt_psum, 1)

            def products(dst, hi_w, lo_w, hi_x, lo_x):
                for ko in range(KO):
                    for j, (w, x) in enumerate(((hi_w, hi_x), (hi_w, lo_x), (lo_w, hi_x))):
                        last = nc.tensor.matmul(dst, w(ko), x(ko), start=(ko == 0 and j == 0),
                                                stop=(ko == KO - 1 and j == 2))
                return last

            pe.wait_ge(w_ready, 3)
            for n, (c, k) in enumerate(QK):
                pe.wait_ge(xt_ready, max(KO * (c + 1), min(n + 1, KO * CH)))
                if n >= 8:
                    pe.wait_ge(squares_ready, n - 7)
                    pe.wait_ge(rest_ready, n - 7)
                i, m = k // 2, k % 2
                products(ps[:, n % 8, :],
                         lambda ko: w_hi[:, i, ko, m * P:(m + 1) * P], lambda ko: w_lo[:, i, ko, m * P:(m + 1) * P],
                         lambda ko: xt_hi[:, ko, c * CW:(c + 1) * CW], lambda ko: xt_lo[:, ko, c * CW:(c + 1) * CW]
                         ).then_inc(proj_psum, 1)

            def project_v(n):
                if n < 4:
                    pe.wait_ge(rest_ready, 8 + V_BANK + n + 1)
                else:
                    pe.wait_ge(v_ready, n - 3)
                for a in range(2):
                    t = 2 * n + a
                    last = products(ps[:, V_BANK + n % 4, a * HID:(a + 1) * HID],
                                    lambda ko: xt_hi[:, ko, t * P:(t + 1) * P],
                                    lambda ko: xt_lo[:, ko, t * P:(t + 1) * P],
                                    lambda ko: w_hi[:, 2, ko, :], lambda ko: w_lo[:, 2, ko, :])
                last.then_inc(proj_psum, 1)

            project_v(0)
            project_v(1)
            pe.wait_ge(squares_ready, len(QK))
            pe.wait_ge(rest_ready, 12)
            for k in range(4):
                for c in range(CH):
                    last = nc.tensor.matmul(ps[32 * c:32 * c + 32, k, :], head_sum[:],
                                            squares[:, k, c * CW:(c + 1) * CW], start=True, stop=True)
            last.then_inc(norms_psum, 1)
            for n in VP[2:]:
                project_v(n)

            pe.wait_ge(flag_ready, 1)
            need_exact = pe.value_load(exact_flag[0:1, 0:1], min_val=0, max_val=1)
            with pe.If(need_exact > 0):
                with pe.Fori(0, NH) as h:
                    pe.wait_ge(gen_loaded, (h + 1) * STACK)
                    for t in range(TT):
                        pe.wait_ge(gen_max, h * TT + t + 1)
                        for b in range(CH):
                            last = nc.tensor.matmul(ps[:, 4 * (t % 2) + b, :], q_stack[0][0:SROW, t * P:(t + 1) * P],
                                                    k_stack[0][0:SROW, b * CW:(b + 1) * CW], start=True, stop=True)
                        last.then_inc(gen_scores, 1)
                pe.wait_ge(gen_max, NH * TT + 2)
                for a in range(2):
                    nc.tensor.transpose(ps[:, 0, a * P:(a + 1) * P],
                                        row_max[:].rearrange("p h (b a) -> p (h b) a", a=2)[:, :, a], ident[:]
                                        ).then_inc(gen_turned, 1)

            def prob_times_v(slot, n, kt):
                for q in range(CH):
                    last = nc.tensor.matmul(ps[32 * q:32 * q + VW, ACC, :], v_slot[slot][:, kt, :],
                                            probs[:, n % 3, q, :], start=(kt == 0), stop=(kt == TT - 1))
                last.then_inc(pv_done, 1)

            def head(h, j, i):
                slot, first = j % 3, (j == 0)
                for kt in range(TT):
                    u = h * TT + kt
                    n = j * TT + kt
                    if kt == 0:
                        pe.wait_ge(stack_loaded[slot], (i + 1 + j // 3) * (STACK + SHIFT))
                    for half in range(2):
                        ring = (2 * n + half) % 3
                        if not (first and 2 * kt + half < 3):
                            pe.wait_ge(exp_done, 2 * u + half - 2)
                        for q in (2 * half, 2 * half + 1):
                            last = nc.tensor.matmul(ps[:, 2 * ring + q % 2, :],
                                                    k_stack[slot][0:ROWS, kt * P:(kt + 1) * P],
                                                    q_stack[slot][0:ROWS, q * CW:(q + 1) * CW], start=True, stop=True)
                        last.then_inc(scores_ready, 1)
                    if kt >= 2:
                        if kt == 2:
                            pe.wait_ge(v_slot_ready, h + 1)
                            if not first:
                                pe.wait_ge(attn_saved, h)
                        pe.wait_ge(exp_done, 2 * (u - 1))
                        prob_times_v(slot, n - 2, kt - 2)
                    elif not first:
                        pe.wait_ge(exp_done, 2 * (u - 1))
                        prob_times_v((j - 1) % 3, n - 2, TT - 2 + kt)

            pe.wait_ge(shift_ready, 1)
            head(0, 0, 0)
            with pe.Fori(0, (NH - 1) // 3) as i:
                for j in range(1, 4):
                    head(i * 3 + j, j, i)
            for kt in (TT - 2, TT - 1):
                pe.wait_ge(exp_done, 2 * ((NH - 1) * TT + kt + 1))
                prob_times_v(0, 3 * TT + kt, kt)

            pe.wait_ge(attn_saved, NH)
            for g in range(8):
                ko, ug, b = g % 2, g // 2, 2 * (g % 3)
                if g >= 3:
                    pe.wait_ge(attn_scaled, g - 2)
                for k in range(8):
                    last = nc.tensor.transpose(
                        ps[:, b + k // 4, (k % 4) * P:(k % 4 + 1) * P],
                        attn[:, 8 * ug + k, HPB * ko:HPB * (ko + 1), :].rearrange("p r h -> p (r h)"), ident[:])
                last.then_inc(attn_turned, 1)
            pe.wait_ge(attn_scaled, 8)
            pe.wait_ge(w_loaded[3], 16)
            for t in range(TT):
                d = t
                for ko in range(KO):
                    last = nc.tensor.matmul(ps[:, t // 2, (t % 2) * HID:(t % 2 + 1) * HID],
                                            at32[:, ko, d, :, :].rearrange("p j u -> p (j u)"), wo[:, ko, :],
                                            start=(ko == 0), stop=(ko == KO - 1))
                if t % 2:
                    last.then_inc(wo_psum, 1)
            for c in range(CH):
                pe.wait_ge(ln1_ready, TPC * (c + 1))
                for ko in range(KO):
                    for i in range(TPC):
                        last = nc.tensor.transpose(ps[:, KO * c + ko, i * P:(i + 1) * P],
                                                   x_tok[:, TPC * c + i, ko * P:(ko + 1) * P], ident[:])
                    last.then_inc(yt_psum, 1)
            pe.wait_ge(yt_ready, KO * CH)
            pe.wait_ge(ffn_w_ready, 3)

            def down(m):
                for i in range(TPC):
                    for j, h in enumerate((h_hi, h_lo)):
                        last = nc.tensor.matmul(ps[:, 4 + i, 0:HID], h[:, m, i * P:(i + 1) * P], wd[:, m, :],
                                                start=(m == 0 and j == 0), stop=(m == MT - 1 and j == 1))
                    if m == MT - 1:
                        last.then_inc(down_psum, 1)

            def ffn_chunk(c, first):
                for m in range(MT):
                    pe.wait_ge(gate_up_free, c * MT + m + 1)
                    for w, bank in ((wg, m % 2), (wu, 2 + m % 2)):
                        for ko in range(KO):
                            for j, y in enumerate((yt_hi, yt_lo)):
                                last = nc.tensor.matmul(ps[:, bank, :], w[:, ko, m * P:(m + 1) * P],
                                                        y[:, ko, bass.ds(c * CW, CW)],
                                                        start=(ko == 0 and j == 0), stop=(ko == KO - 1 and j == 1))
                    last.then_inc(gate_up_psum, 1)
                    if m >= 2 or not first:
                        pe.wait_ge(h_ready, c * MT + m + 1)
                        if m == 2:
                            pe.wait_ge(down_free, (c + 1) * TPC)
                        down((m - 2) % MT)

            ffn_chunk(0, True)
            with pe.Fori(1, CH) as c:
                ffn_chunk(c, False)
            for m in (MT - 2, MT - 1):
                pe.wait_ge(h_ready, (CH - 1) * MT + m + 3)
                down(m)


_INS = ['L0_attn_X', 'L0_attn_Wq', 'L0_attn_bq', 'L0_attn_Wk', 'L0_attn_bk', 'L0_attn_Wv', 'L0_attn_bv', 'L0_attn_Wo',
        'L0_attn_bo', 'L0_ffn_w_gate', 'L0_ffn_w_up', 'L0_ffn_w_down', 'L0_ffn_s_gate', 'L0_ffn_s_up', 'L0_ffn_s_down']


def kernel(**inputs):
    import concourse.bacc as _bacc
    from concourse.bass_utils import run_bass_kernel_spmd as _run

    nc = _bacc.Bacc("TRN2", target_bir_lowering=False, num_devices=1)
    arrays, args = {}, []
    for name in _INS:
        a = np.ascontiguousarray(inputs[name])
        if a.dtype == np.int8:
            a = a.view(np.int32)
        arrays[f"in_{name}"] = a
        args.append(nc.dram_tensor(f"in_{name}", a.shape, mybir.dt.from_np(a.dtype), kind="ExternalInput").ap())
    shape = np.shape(inputs['L0_attn_X'])
    args.append(nc.dram_tensor("out_0", shape, mybir.dt.float32, kind="ExternalOutput").ap())
    layer_program(nc, *args)
    r = _run(nc, [arrays], core_ids=[0])
    return r.results[0]["out_0"]
```

```python
import numpy as np
import concourse.bass as bass
from concourse import mybir
from contextlib import ExitStack


def layer_program(nc, X, Wq, bq, Wk, bk, Wv, bv, Wo, bo, w_gate, w_up, w_down, s_gate, s_up, s_down, out):
    f32, f32r, bf16 = mybir.dt.float32, mybir.dt.float32r, mybir.dt.bfloat16
    i8, i32 = mybir.dt.int8, mybir.dt.int32
    ALU = mybir.AluOpType
    ACT = mybir.ActivationFunctionType
    AXX = mybir.AxisListType.X
    MAX_ACROSS = bass.bass_isa.ReduceOp.max

    P = 128
    S, HID = X.shape[1], X.shape[2]
    NH = 16
    HD = HID // NH
    INTER = s_gate.shape[0]
    KO = HID // P
    TT = S // P
    CW = 512
    CH = S // CW
    TPC = TT // CH
    MT = INTER // P
    HPB = P // HD
    PRODUCTS = [(3, 0, 0), (2, 1, 0), (1, 2, 0)]
    SROW = sum(n for n, _, _ in PRODUCTS) * HD
    MROW = SROW + 1
    ROWS = MROW + 3
    LAG = 3
    VW = 32
    NSLOT = 3
    SCALE = float(HD) ** -0.5
    SAFE = 40.0
    EPS = 1e-5

    with ExitStack() as ctx:
        arena_at = (nc.sbuf_base + 63) // 64 * 64
        place_at = [arena_at]

        def place(name, shape, dt, at=None):
            size = int(np.prod(shape[1:])) * {f32: 4, f32r: 4, i32: 4, bf16: 2, i8: 1}[dt]
            where = place_at[0] if at is None else at
            if at is None:
                place_at[0] += (size + 63) // 64 * 64
            return nc.alloc_sbuf_tensor_at(name, shape, dt, offset=where)

        def region(size):
            at = place_at[0]
            place_at[0] += size
            return at

        KB = 1024
        x_tok = place("x_tok", [P, TT, HID], f32)
        gate8 = place("gate8", [P, KO, INTER // 4], i32)
        up8 = place("up8", [P, KO, INTER // 4], i32)
        down8 = place("down8", [P, MT, HID // 4], i32)
        wo = place("wo", [P, KO, HID], f32)
        ident = place("ident", [P, P], f32)
        head_sum = place("head_sum", [P, 32], bf16)
        bq_c = place("bq_c", [P, KO], f32)
        bk_c = place("bk_c", [P, KO], f32)
        bv_b = place("bv_b", [P, HID], f32)
        bo_b = place("bo_b", [P, HID], f32)
        sdown_b = place("sdown_b", [P, HID], f32)
        sgate_c = place("sgate_c", [P, MT], f32)
        sup_c = place("sup_c", [P, MT], f32)
        norm_max = place("norm_max", [P, 4], f32)
        norm_qk = place("norm_qk", [P, 2], f32)
        norm_all = place("norm_all", [P, 2], f32)
        norm_sum = place("norm_sum", [P, 1], f32)
        norm_ok = place("norm_ok", [P, 1], f32)
        bound_neg = place("bound_neg", [P, 1], f32)
        ones_row = place("ones_row", [HPB, 2 * P], bf16)
        exact_flag = place("exact_flag", [P, 1], i32)
        row_max = place("row_max", [P, NH, TT], f32)
        shift = place("shift", [P, 3, 2 * P], bf16)
        shift_rest = place("shift_rest", [P, 2 * P], f32)
        den = place("den", [P, 4, 8, 4], f32)
        stats = place("stats", [P, TT, 6], f32)
        mean_var = place("mean_var", [P, TT, 2], f32)
        var_eps = place("var_eps", [P, TPC], f32)
        rstd = place("rstd", [P, TT], f32)
        neg_mean = place("neg_mean", [P, TT], f32)
        warm = place("warm", [P, TPC], f32)
        minus_half = place("minus_half", [P, TPC], f32)
        q_stack = [place(f"q_stack{i}", [ROWS, S], bf16) for i in range(NSLOT)]
        k_stack = [place(f"k_stack{i}", [ROWS, S], bf16) for i in range(NSLOT)]
        v_slot = [place(f"v_slot{i}", [P, TT, VW], f32) for i in range(NSLOT)]

        at = region(16 * KB)
        v_all = place("v_all", [P, TT, HID], f32, at)
        wd = place("wd", [P, MT, HID], f32r, at)
        h32 = place("h32", [P, 2, CW], f32, at + 8 * KB)
        sg = place("sg", [P, 2, CW], f32, at + 12 * KB)
        at = region(42 * KB)
        w_raw = place("w_raw", [P, 3, KO * HID], f32, at)
        w_hi = place("w_hi", [P, 3, KO, HID], f32r, at + 6 * KB)
        w_lo = place("w_lo", [P, 3, KO, HID], f32r, at + 12 * KB)
        rest = place("rest", [P, 4, CW], f32, at + 18 * KB)
        squares = place("squares", [P, 4, S], bf16, at + 26 * KB)
        attn = place("attn", [P, S // NH // 4, NH, NH], f32, at)
        h_hi = place("h_hi", [P, MT, CW], f32r, at)
        h_lo = place("h_lo", [P, MT, CW], f32r, at + 16 * KB)
        r_tmp = place("r_tmp", [P, TPC, HID], f32, at + 34 * KB)
        at = region(48 * KB)
        q_parts = place("q_parts", [P, KO, 3, S], bf16, at)
        k_parts = place("k_parts", [P, KO, 3, S], bf16, at + 24 * KB)
        at32 = place("at32", [P, KO, HD, 4, 32], f32, at)
        out_tmp = place("out_tmp", [P, TPC, HID], f32, at + 16 * KB)
        wg = place("wg", [P, KO, INTER], f32r, at + 32 * KB)
        wu = place("wu", [P, KO, INTER], f32r, at + 40 * KB)
        at = region(32 * KB)
        xt_hi = place("xt_hi", [P, KO, S], f32r, at)
        xt_lo = place("xt_lo", [P, KO, S], f32r, at + 16 * KB)
        probs = place("probs", [P, 3, CH, CW], f32, at)
        yt_hi = place("yt_hi", [P, KO, S], f32r, at)
        yt_lo = place("yt_lo", [P, KO, S], f32r, at + 16 * KB)

        ps = ctx.enter_context(nc.psum_tensor("ps", [P, 8, CW], f32))
        ACC = 6

        def sem(name):
            return ctx.enter_context(nc.semaphore(name))

        x_loaded = [sem(f"x_loaded{c}") for c in range(CH)]
        x_half_loaded = sem("x_half_loaded")
        w_loaded = [sem(f"w_loaded{i}") for i in range(4)]
        bias_loaded = sem("bias_loaded")
        bv_loaded = sem("bv_loaded")
        bo_loaded = sem("bo_loaded")
        scales_loaded = sem("scales_loaded")
        late_loaded = sem("late_loaded")
        consts_ready = sem("consts_ready")
        pool_step = sem("pool_step")
        dve_step = sem("dve_step")
        pad_ready = sem("pad_ready")
        ones_ready = sem("ones_ready")
        ones_pool = sem("ones_pool")
        warm_ready = sem("warm_ready")
        w_hi_ready = sem("w_hi_ready")
        w_ready = sem("w_ready")
        xt_psum = sem("xt_psum")
        xt_hi_ready = sem("xt_hi_ready")
        xt_ready = sem("xt_ready")
        proj_psum = sem("proj_psum")
        v_psum = sem("v_psum")
        part1_ready = sem("part1_ready")
        squares_ready = sem("squares_ready")
        rest_ready = sem("rest_ready")
        part2_pool = sem("part2_pool")
        part2_dve = sem("part2_dve")
        part3_ready = sem("part3_ready")
        v_ready = sem("v_ready")
        norms_psum = sem("norms_psum")
        norms_ready = sem("norms_ready")
        norms_reduced = sem("norms_reduced")
        flag_ready = sem("flag_ready")
        gen_loaded = sem("gen_loaded")
        gen_scores = sem("gen_scores")
        gen_max = sem("gen_max")
        gen_turned = sem("gen_turned")
        gen_split = sem("gen_split")
        gen_reloaded = sem("gen_reloaded")
        shift_zero = sem("shift_zero")
        ones_loaded = sem("ones_loaded")
        bound_ready = sem("bound_ready")
        bound_zero = sem("bound_zero")
        stack_loaded = [sem(f"stack_loaded{i}") for i in range(NSLOT)]
        v_slot_ready = sem("v_slot_ready")
        scores_ready = sem("scores_ready")
        exp_done = sem("exp_done")
        pv_done = sem("pv_done")
        attn_saved = sem("attn_saved")
        ffn_w_ready = sem("ffn_w_ready")
        bo_added = sem("bo_added")
        attn_turned = sem("attn_turned")
        den_ready = sem("den_ready")
        attn_scaled = sem("attn_scaled")
        wo_psum = sem("wo_psum")
        ln1_sum = sem("ln1_sum")
        ln1_var = sem("ln1_var")
        ln1_rstd = sem("ln1_rstd")
        ln1_mean = sem("ln1_mean")
        ln1_ready = sem("ln1_ready")
        yt_psum = sem("yt_psum")
        yt_hi_ready = sem("yt_hi_ready")
        yt_ready = sem("yt_ready")
        gate_up_psum = sem("gate_up_psum")
        gate_up_free = sem("gate_up_free")
        silu_done = sem("silu_done")
        h_hi_ready = sem("h_hi_ready")
        h_ready = sem("h_ready")
        down_psum = sem("down_psum")
        down_free = sem("down_free")
        ln2_sum = sem("ln2_sum")
        ln2_stat = sem("ln2_stat")
        ln2_gate = sem("ln2_gate")
        ln2_aggr = sem("ln2_aggr")
        ln2_var = sem("ln2_var")
        ln2_rstd = sem("ln2_rstd")
        ln2_ready = sem("ln2_ready")
        tail_sum = sem("tail_sum")
        tail_mean = sem("tail_mean")
        tail_scaled = sem("tail_scaled")
        stored = sem("stored")

        block = ctx.enter_context(nc.Block())

        x_view = X.rearrange("a (t p) n -> p (a t) n", p=P)
        out_view = out.rearrange("a (t p) n -> p (a t) n", p=P)
        STACK = 16 * 2 * len(PRODUCTS)
        SHIFT = 16 * 3
        YT_BANK = [0, 4, 6, 4]
        FIRST_DOWN = {4: (0,), 5: (1,), 6: (2, 3), 7: (4,)}

        QK = [(c, k) for c in range(CH) for k in (0, 2, 1, 3)]
        QK_BANKS = 4
        X_BANK = 6
        WARM_BANK, WARM_BEFORE, WARM_BEHIND = 5, 10, 8
        V_AFTER = [(0, 1), (2, 3), (4,), (5, 6, 7)]
        V_BANK = [4, 5, 4, 5, 4, 5, 4, 2]
        NORM_BANK = [6, 7, 0, 1]

        @block.sync
        def _(sp):
            def load_weight(i, w):
                sp.dma_start(w_raw[:, i, :].rearrange("p (k n) -> p k n", k=KO),
                             w.rearrange("(k p) n -> p k n", p=P)).then_inc(w_loaded[i], 16)

            def load_x(c):
                sp.dma_start(x_tok[:, TPC * c:TPC * (c + 1), :], x_view[:, TPC * c:TPC * (c + 1), :]
                             ).then_inc(x_loaded[c], 16)

            half = TPC // 2
            sp.dma_start(x_tok[:, 0:half, :], x_view[:, 0:half, :]).then_inc(x_half_loaded, 16)
            sp.dma_start(x_tok[:, half:TPC, :], x_view[:, half:TPC, :]).then_inc(x_loaded[0], 16)
            load_weight(1, Wk)
            load_x(1)
            load_weight(2, Wv)
            load_x(2)
            load_x(3)
            sp.dma_start(bv_b[:], bv.partition_broadcast(P)).then_inc(bv_loaded, 16)
            sp.dma_start(bo_b[:], bo.partition_broadcast(P)).then_inc(bo_loaded, 16)
            sp.dma_start(wo[:], Wo.rearrange("(k p) n -> p k n", p=P)).then_inc(w_loaded[3], 16)
            sp.dma_start(sdown_b[:], s_down.partition_broadcast(P)).then_inc(scales_loaded, 16)
            sp.dma_start(sgate_c[:], s_gate.rearrange("(k p) -> p k", p=P),
                         allow_slow_non_contiguous=True).then_inc(scales_loaded, 16)
            sp.dma_start(sup_c[:], s_up.rearrange("(k p) -> p k", p=P),
                         allow_slow_non_contiguous=True).then_inc(scales_loaded, 16)
            sp.dma_start(gate8[:], w_gate.rearrange("(k p) n -> p k n", p=P)).then_inc(late_loaded, 16)
            sp.dma_start(up8[:], w_up.rearrange("(k p) n -> p k n", p=P)).then_inc(late_loaded, 16)
            sp.dma_start(down8[:], w_down.rearrange("(k p) n -> p k n", p=P)).then_inc(late_loaded, 16)

            def load_q(h, slot, product, done):
                n, part, _ = PRODUCTS[product]
                at, row = HD * sum(p[0] for p in PRODUCTS[:product]), HD * (h % HPB)
                sp.dma_start(q_stack[slot][at:at + n * HD, :],
                             q_parts[row:row + HD, h // HPB, part:part + 1, :].to_broadcast([HD, n, S])
                             ).then_inc(done, 16)

            def load_k(h, slot, product, done):
                n, _, part = PRODUCTS[product]
                at, row = HD * sum(p[0] for p in PRODUCTS[:product]), HD * (h % HPB)
                sp.dma_start(k_stack[slot][at:at + n * HD, :],
                             k_parts[row:row + HD, h // HPB, part:part + n, :]).then_inc(done, 16)

            def load_stack(h, slot, done):
                for product in range(len(PRODUCTS)):
                    load_q(h, slot, product, done)
                    load_k(h, slot, product, done)

            def load_shift(h, slot, done):
                for i in range(3):
                    sp.dma_start(q_stack[slot][MROW + i:MROW + i + 1, :],
                                 shift[h * HPB:(h + 1) * HPB, i, :]).then_inc(done, 16)

            def refill(h, slot):
                sp.wait_ge(scores_ready, (h - NSLOT + 1) * 2 * TT)
                load_stack(h, slot, stack_loaded[slot])
                load_shift(h, slot, stack_loaded[slot])

            sp.wait_ge(shift_zero, 2)
            for s in range(NSLOT):
                sp.dma_start(q_stack[s][SROW:MROW, :], ones_row[:]).then_inc(ones_loaded, 16)
            load_shift(0, 0, stack_loaded[0])
            sp.wait_ge(part1_ready, len(QK) - 2)
            load_q(0, 0, 0, stack_loaded[0])
            load_k(0, 0, 2, stack_loaded[0])
            sp.wait_ge(part2_pool, len(QK) // 2 - 1)
            load_q(0, 0, 1, stack_loaded[0])
            sp.wait_ge(part2_dve, len(QK) // 2 - 1)
            load_k(0, 0, 1, stack_loaded[0])
            sp.wait_ge(part3_ready, len(QK) - 4)
            load_k(0, 0, 0, stack_loaded[0])
            sp.wait_ge(part3_ready, len(QK) - 3)
            load_q(0, 0, 2, stack_loaded[0])
            for h in range(1, NSLOT):
                load_stack(h, h, stack_loaded[h])
            sp.wait_ge(part3_ready, len(QK))
            sp.wait_ge(flag_ready, 1)
            need_exact = sp.value_load(exact_flag[0:1, 0:1], min_val=0, max_val=1)
            with sp.If(need_exact > 0):
                sp.wait_ge(stack_loaded[0], STACK + SHIFT)
                for h in range(NH):
                    if h:
                        sp.wait_ge(gen_max, h * TT + 2)
                    load_stack(h, 0, gen_loaded)
                sp.wait_ge(gen_max, NH * TT + 2)
                load_stack(0, 0, gen_reloaded)
                sp.wait_ge(gen_split, 4)
                load_shift(0, 0, gen_reloaded)
                sp.wait_ge(gen_reloaded, STACK + SHIFT)
            for h in range(1, NSLOT):
                load_shift(h, h, stack_loaded[h])
            for h in range(NSLOT, NH):
                refill(h, h % NSLOT)
            with sp.Fori(0, CH - 1) as c:
                sp.wait_ge(ln2_ready, (c + 1) * TPC)
                sp.dma_start(out_view[:, bass.ds(c * TPC, TPC), :], out_tmp[:]).then_inc(stored, 16)
            for b in range(2):
                t = TT - TPC + 2 * b
                sp.wait_ge(ln2_ready, TT - TPC + b + 1)
                sp.wait_ge(tail_scaled, b + 1)
                sp.dma_start(out_view[:, t:t + 2, :], out_tmp[:, t % TPC:t % TPC + 2, :]).then_inc(stored, 16)
            sp.wait_ge(stored, 16 * (CH + 2))

        @block.gpsimd
        def _(pool):
            steps = [0]

            def then(instruction):
                steps[0] += 1
                instruction.then_inc(pool_step, 1)
                pool.wait_ge(pool_step, steps[0])

            then(nc.gpsimd.memset(ident[:], 0.0))
            nc.gpsimd.affine_select(out=ident[:], in_=ident[:], compare_op=ALU.not_equal, fill=1.0, base=0,
                                    pattern=[[-1, P]], channel_multiplier=1).then_inc(consts_ready, 1)
            then(nc.gpsimd.memset(head_sum[:], 1.0))
            then(nc.gpsimd.affine_select(out=head_sum[:], in_=head_sum[:], compare_op=ALU.is_ge, fill=0.0, base=0,
                                         pattern=[[-HD, 32]], channel_multiplier=1))
            nc.gpsimd.affine_select(out=head_sum[:], in_=head_sum[:], compare_op=ALU.is_ge, fill=0.0, base=HD - 1,
                                    pattern=[[HD, 32]], channel_multiplier=-1).then_inc(consts_ready, 1)
            nc.gpsimd.memset(minus_half[:], -0.5).then_inc(warm_ready, 1)
            pool.wait_ge(warm_ready, 1)
            nc.gpsimd.memset(k_stack[2][SROW:ROWS, :], 1.0).then_inc(ones_pool, 1)
            pool.wait_ge(ones_pool, 1)
            for s in range(NSLOT):
                then(nc.gpsimd.memset(v_slot[s][:], 0.0))
                nc.gpsimd.memset(v_slot[s][:, :, HD:HD + 1], 1.0).then_inc(pad_ready, 1)
            for n in range(0, len(QK), 2):
                c, k = QK[n]
                parts = q_parts if k < 2 else k_parts
                pool.wait_ge(rest_ready, n + 1)
                nc.gpsimd.tensor_copy(parts[:, k % 2, 1, c * CW:(c + 1) * CW], rest[:, n % 4, :]
                                      ).then_inc(part2_pool, 1)
            pool.wait_ge(norms_ready, 3)
            nc.gpsimd.partition_all_reduce(norm_all[:], norm_qk[:], P, MAX_ACROSS).then_inc(norms_reduced, 1)
            pool.wait_ge(bo_loaded, 16)
            pool.wait_ge(xt_ready, 2 * CH)
            for t in range(0, TT, 2):
                nc.gpsimd.tensor_tensor(x_tok[:, t:t + 2, :], x_tok[:, t:t + 2, :],
                                        bo_b[:].unsqueeze(1).to_broadcast([P, 2, HID]), ALU.add
                                        ).then_inc(bo_added, 1)
            pool.wait_ge(late_loaded, 16 * 3)
            for s in range(NSLOT):
                pool.wait_ge(stack_loaded[s], len(range(s, NH, NSLOT)) * (STACK + SHIFT))
            nc.gpsimd.tensor_copy(wg[:], gate8[:].bitcast(i8)).then_inc(ffn_w_ready, 1)
            nc.gpsimd.tensor_copy(wu[:], up8[:].bitcast(i8)).then_inc(ffn_w_ready, 1)
            pool.wait_ge(v_slot_ready, NH)
            nc.gpsimd.tensor_copy(wd[:], down8[:].bitcast(i8)).then_inc(ffn_w_ready, 1)
            pool.wait_ge(warm_ready, 1)
            for c in range(CH):
                pool.wait_ge(ln1_var, c + 1)
                nc.gpsimd.tensor_tensor(rstd[:, TPC * c:TPC * (c + 1)], var_eps[:], minus_half[:], ALU.pow
                                        ).then_inc(ln1_rstd, 1)
            with pool.Fori(0, CH - 1) as c:
                pool.wait_ge(ln2_var, c + 1)
                nc.gpsimd.tensor_tensor(rstd[:, 0:TPC], var_eps[:], minus_half[:], ALU.pow).then_inc(ln2_rstd, 1)
            pool.wait_ge(down_free, CH * TPC + 1)
            nc.gpsimd.tensor_tensor(r_tmp[:, 0:2, :], r_tmp[:, 0:2, :], x_tok[:, TT - 4:TT - 2, :], ALU.add
                                    ).then_inc(tail_sum, 1)
            for b in range(2):
                pool.wait_ge(ln2_var, CH + b)
                nc.gpsimd.tensor_tensor(rstd[:, 2 * b:2 * b + 2], var_eps[:, 2 * b:2 * b + 2],
                                        minus_half[:, 0:2], ALU.pow).then_inc(ln2_rstd, 1)

        def three_heads(engine, head):
            head(0, 0)
            with engine.Fori(0, (NH - 1) // 3) as i:
                for j in range(1, 4):
                    head(i * 3 + j, j)

        @block.scalar
        def _(act):
            act.dma_start(w_raw[:, 0, :].rearrange("p (k n) -> p k n", k=KO),
                          Wq.rearrange("(k p) n -> p k n", p=P)).then_inc(w_loaded[0], 16)
            act.dma_start(bq_c[:], bq.rearrange("(k p) -> p k", p=P),
                          allow_slow_non_contiguous=True).then_inc(bias_loaded, 16)
            act.dma_start(bk_c[:], bk.rearrange("(k p) -> p k", p=P),
                          allow_slow_non_contiguous=True).then_inc(bias_loaded, 16)
            act.wait_ge(warm_ready, 1)
            nc.scalar.activation(warm[:], minus_half[:], ACT.Exp).then_inc(warm_ready, 1)

            def hi_of_w(i):
                act.wait_ge(w_loaded[i], 16)
                nc.scalar.copy(w_hi[:, i, :, :], w_raw[:, i, :].rearrange("p (k n) -> p k n", k=KO)
                               ).then_inc(w_hi_ready, 1)

            def hi_of_x(c):
                for ko in range(KO):
                    t = KO * c + ko
                    act.wait_ge(xt_psum, t + 1)
                    nc.scalar.copy(xt_hi[:, ko, c * CW:(c + 1) * CW], ps[:, X_BANK + ko, :]
                                   ).then_inc(xt_hi_ready, 1)

            hi_of_w(0)
            hi_of_x(0)
            hi_of_w(1)
            hi_of_w(2)
            for n, (c, k) in enumerate(QK):
                parts, b_c = (q_parts, bq_c) if k < 2 else (k_parts, bk_c)
                if n == 0:
                    act.wait_ge(bias_loaded, 16 * 2)
                act.wait_ge(proj_psum, n + 1)
                nc.scalar.activation(parts[:, k % 2, 0, c * CW:(c + 1) * CW], ps[:, n % QK_BANKS, :], ACT.Identity,
                                     bias=b_c[:, k % 2:k % 2 + 1]).then_inc(part1_ready, 1)
                nc.scalar.activation(squares[:, k, c * CW:(c + 1) * CW], ps[:, n % QK_BANKS, :], ACT.Square,
                                     bias=b_c[:, k % 2:k % 2 + 1]).then_inc(squares_ready, 1)
                if n % 4 == 1 and c + 1 < CH:
                    hi_of_x(c + 1)
                if n % 4 == 3:
                    for p in V_AFTER[c]:
                        act.wait_ge(v_psum, p + 1)
                        nc.scalar.copy(v_all[:, 2 * p:2 * p + 2, :],
                                       ps[:, V_BANK[p], :].rearrange("p (a b) -> p a b", a=2)).then_inc(v_ready, 1)

            def head(h, j):
                for kt in range(TT):
                    u = h * TT + kt
                    for half in range(2):
                        ring = (2 * (j * TT + kt) + half) % 3
                        act.wait_ge(scores_ready, 2 * u + half + 1)
                        if half == 0 and not (j == 0 and kt < 3):
                            act.wait_ge(pv_done, u - 2)
                        nc.scalar.activation(
                            probs[:, (j * TT + kt) % 3, 2 * half:2 * half + 2, :].rearrange("p a b -> p (a b)"),
                            ps[:, 2 * ring:2 * ring + 2, :].rearrange("p a b -> p (a b)"),
                            ACT.Exp, bias=0.0, scale=SCALE).then_inc(exp_done, 1)

            act.wait_ge(xt_ready, 2 * CH)
            three_heads(act, head)
            act.wait_ge(warm_ready, 2)
            nc.scalar.activation(warm[:], minus_half[:], ACT.Silu)

            def ln1_scale(c):
                act.wait_ge(ln1_mean, c + 1)
                for t in range(TPC * c, TPC * (c + 1)):
                    nc.scalar.activation(x_tok[:, t, :], x_tok[:, t, :], ACT.Identity, scale=rstd[:, t:t + 1],
                                         bias=neg_mean[:, t:t + 1]).then_inc(ln1_ready, 1)

            def ln1_hi(c):
                for ko in range(KO):
                    act.wait_ge(yt_psum, KO * c + ko + 1)
                    nc.scalar.copy(yt_hi[:, ko, c * CW:(c + 1) * CW], ps[:, YT_BANK[c] + ko, :]
                                   ).then_inc(yt_hi_ready, 1)

            ln1_scale(0)
            ln1_scale(1)
            ln1_hi(0)
            ln1_scale(2)
            act.wait_ge(scales_loaded, 16 * 3)

            def ffn_chunk(c, first):
                for m in range(MT + 1):
                    if m < MT:
                        u = c * MT + m
                        act.wait_ge(gate_up_psum, u + 1)
                        act.wait_ge(gate_up_free, u + 1)
                        nc.scalar.activation(sg[:, m % 2, :], ps[:, m % 2, :], ACT.Silu,
                                             scale=sgate_c[:, m:m + 1]).then_inc(silu_done, 1)
                    if first and m == 0:
                        ln1_hi(1)
                        ln1_scale(3)
                    if m > 0:
                        act.wait_ge(gate_up_free, c * MT + m + 2)
                        nc.scalar.copy(h_hi[:, m - 1, :], h32[:, (m - 1) % 2, :]).then_inc(h_hi_ready, 1)
                    if first and m == 1:
                        ln1_hi(2)
                    if first and m == 2:
                        ln1_hi(3)

            ffn_chunk(0, True)
            with act.Fori(1, CH) as c:
                ffn_chunk(c, False)
            act.wait_ge(stored, CH * 16)
            for b in range(2):
                i = 2 * b
                act.wait_ge(tail_mean, b + 1)
                nc.scalar.activation(out_tmp[:, i, :], r_tmp[:, i, :], ACT.Identity, scale=rstd[:, i:i + 1],
                                     bias=neg_mean[:, i:i + 1]).then_inc(tail_scaled, 1)

        @block.vector
        def _(dve):
            steps = [0]

            def then(instruction):
                steps[0] += 1
                instruction.then_inc(dve_step, 1)
                dve.wait_ge(dve_step, steps[0])

            nc.vector.memset(shift[:], 0.0).then_inc(shift_zero, 1)
            nc.vector.memset(ones_row[:], 1.0).then_inc(shift_zero, 1)

            def write_ones(slot):
                nc.vector.memset(k_stack[slot][SROW:ROWS, :], 1.0).then_inc(ones_ready, 1)

            write_ones(0)

            def lo_of_w(i):
                dve.wait_ge(w_hi_ready, i + 1)
                nc.vector.tensor_tensor(w_lo[:, i, :, :], w_raw[:, i, :].rearrange("p (k n) -> p k n", k=KO),
                                        w_hi[:, i, :, :].bitcast(f32), ALU.subtract).then_inc(w_ready, 1)

            def lo_of_x(c):
                for ko in range(KO):
                    dve.wait_ge(xt_hi_ready, KO * c + ko + 1)
                    nc.vector.tensor_tensor(xt_lo[:, ko, c * CW:(c + 1) * CW], ps[:, X_BANK + ko, :],
                                            xt_hi[:, ko, c * CW:(c + 1) * CW].bitcast(f32), ALU.subtract
                                            ).then_inc(xt_ready, 1)

            def second_part(n):
                c, k = QK[n]
                parts = q_parts if k < 2 else k_parts
                dve.wait_ge(rest_ready, n + 1)
                nc.vector.tensor_copy(parts[:, k % 2, 1, c * CW:(c + 1) * CW], rest[:, n % 4, :]
                                      ).then_inc(part2_dve, 1)

            def third_part(n):
                c, k = QK[n]
                parts = q_parts if k < 2 else k_parts
                dve.wait_ge(part2_dve if n % 2 else part2_pool, n // 2 + 1)
                nc.vector.tensor_tensor(parts[:, k % 2, 2, c * CW:(c + 1) * CW], rest[:, n % 4, :],
                                        parts[:, k % 2, 1, c * CW:(c + 1) * CW], ALU.subtract
                                        ).then_inc(part3_ready, 1)

            lo_of_w(0)
            lo_of_x(0)
            lo_of_w(1)
            lo_of_w(2)
            write_ones(1)

            def rest_of(n):
                c, k = QK[n]
                parts, b_c = (q_parts, bq_c) if k < 2 else (k_parts, bk_c)
                dve.wait_ge(squares_ready, n + 1)
                if n >= 4:
                    dve.wait_ge(part3_ready, n - 3 if n < LAST else LAST - 1)
                nc.vector.scalar_tensor_tensor(rest[:, n % 4, :], ps[:, n % QK_BANKS, :], b_c[:, k % 2:k % 2 + 1],
                                               parts[:, k % 2, 0, c * CW:(c + 1) * CW], ALU.add, ALU.subtract
                                               ).then_inc(rest_ready, 1)

            LAST = len(QK) - 1
            for n in range(LAST):
                c = QK[n][0]
                rest_of(n)
                if n % 4 == 1 and c + 1 < CH:
                    lo_of_x(c + 1)
                if n % 2:
                    second_part(n)
                if n == LAST - 2:
                    third_part(n)
                elif n >= 2:
                    third_part(n - 2)
            for b in range(2):
                dve.wait_ge(norms_psum, b + 1)
                nc.vector.reduce_max(norm_max[:, 2 * b:2 * b + 2], ps[:, NORM_BANK[2 * b]:NORM_BANK[2 * b] + 2, :], AXX
                                     ).then_inc(norms_ready, 1)
            dve.wait_ge(norms_ready, 2)
            nc.vector.tensor_tensor(norm_qk[:], norm_max[:, 0:2], norm_max[:, 2:4], ALU.max).then_inc(norms_ready, 1)

            third_part(LAST - 4)

            dve.wait_ge(norms_reduced, 1)
            then(nc.vector.tensor_tensor(norm_sum[:], norm_all[:, 0:1], norm_all[:, 1:2], ALU.add))
            nc.vector.tensor_scalar(bound_neg[:], norm_sum[:], -0.51, None, ALU.mult).then_inc(norms_ready, 1)
            then(nc.vector.tensor_scalar(norm_ok[:], norm_sum[:], 0.51 * SCALE, SAFE, ALU.mult, ALU.is_le))
            nc.vector.tensor_scalar(exact_flag[:], norm_ok[:], -1.0, 1.0, ALU.mult, ALU.add).then_inc(flag_ready, 1)

            def write_bound(slot, first, last):
                nc.vector.tensor_scalar(k_stack[slot][SROW:MROW, first:last], k_stack[slot][SROW:MROW, first:last],
                                        bound_neg[SROW:MROW, 0:1], None, ALU.mult).then_inc(bound_ready, 1)

            dve.wait_ge(ones_ready, NSLOT - 1)
            dve.wait_ge(norms_ready, 4)
            write_bound(0, 0, 2 * P)
            rest_of(LAST)
            write_bound(0, 2 * P, S)

            def fill_v_slot(h, slot):
                nc.vector.tensor_tensor(v_slot[slot][:, :, 0:HD], v_all[:, :, bass.ds(h * HD, HD)],
                                        bv_b[:, bass.ds(h * HD, HD)].unsqueeze(1).to_broadcast([P, TT, HD]), ALU.add
                                        ).then_inc(v_slot_ready, 1)

            dve.wait_ge(bv_loaded, 16)
            dve.wait_ge(pad_ready, NSLOT)
            dve.wait_ge(v_ready, TT // 2)
            fill_v_slot(0, 0)
            dve.wait_ge(ones_pool, 1)
            for h in range(1, NSLOT):
                write_bound(h, 0, S)
                fill_v_slot(h, h)
            second_part(LAST)
            third_part(LAST - 1)
            third_part(LAST)
            dve.wait_ge(flag_ready, 1)
            need_exact = dve.value_load(exact_flag[0:1, 0:1], min_val=0, max_val=1)
            with dve.If(need_exact > 0):
                dve.wait_ge(bound_ready, NSLOT + 1)
                for s in range(NSLOT):
                    nc.vector.memset(k_stack[s][SROW:MROW, :], 0.0).then_inc(bound_zero, 1)
                dve.sem_inc(gen_max, 2)
                with dve.Fori(0, NH) as h:
                    for t in range(TT):
                        dve.wait_ge(gen_scores, h * TT + t + 1)
                        nc.vector.reduce_max(row_max[:, bass.ds(h, 1), t], ps[:, 4 * (t % 2):4 * (t % 2) + 4, :]
                                             .rearrange("p a b -> p (a b)"), AXX).then_inc(gen_max, 1)
                dve.wait_ge(gen_turned, 2)
                turned = ps[:, 0, 0:2 * P]
                nc.vector.tensor_scalar(shift[:, 0, :], turned, -1.0, None, ALU.mult).then_inc(gen_split, 1)
                dve.wait_ge(gen_split, 1)
                nc.vector.scalar_tensor_tensor(shift_rest[:], turned, -1.0, shift[:, 0, :], ALU.mult, ALU.subtract
                                               ).then_inc(gen_split, 1)
                dve.wait_ge(gen_split, 2)
                nc.vector.tensor_copy(shift[:, 1, :], shift_rest[:]).then_inc(gen_split, 1)
                dve.wait_ge(gen_split, 3)
                nc.vector.tensor_tensor(shift[:, 2, :], shift_rest[:], shift[:, 1, :], ALU.subtract
                                        ).then_inc(gen_split, 1)

            def head(h, j):
                dve.wait_ge(pv_done, (h + 1) * TT)
                nc.vector.tensor_scalar(attn[:, :, :, bass.ds(h, 1)],
                                        ps[:, ACC, :].rearrange("p (u r o) -> p u r o", r=NH, o=1), 1.0, None,
                                        ALU.mult).then_inc(attn_saved, 1)

            def head_and_fill(h, j):
                head(h, j)
                fill_v_slot(h + NSLOT, j % 3)

            head_and_fill(0, 0)
            with dve.Fori(0, (NH - 1) // 3 - 1) as i:
                for j in range(1, 4):
                    head_and_fill(i * 3 + j, j)
            for h in range(NH - NSLOT, NH):
                head(h, h)

            dve.sem_inc(gate_up_free, 2)
            dve.sem_inc(down_free, TPC)
            dve.sem_inc(h_ready, 2)
            dve.sem_inc(stored, 16)

            def turned(g):
                return ps[:, 2 * (g % 4):2 * (g % 4) + 2, :].rearrange("p b (u j d) -> p (b u) j d", u=4, d=32)

            def invert(g):
                dve.wait_ge(attn_turned, g + 1)
                if g >= 4:
                    dve.wait_ge(attn_scaled, g - 3)
                nc.vector.reciprocal(den[:, g % 4, :, :], turned(g)[:, :, :, HD]).then_inc(den_ready, 1)

            invert(0)
            for g in range(8):
                ko, ug = g // 4, g % 4
                if g + 1 < 8:
                    invert(g + 1)
                dve.wait_ge(den_ready, g + 1)
                nc.vector.tensor_tensor(
                    at32[:, ko, :, :, 8 * ug:8 * ug + 8].rearrange("p d j u -> p u j d"), turned(g)[:, :, :, 0:HD],
                    den[:, g % 4, :, :].unsqueeze(3).to_broadcast([P, 8, 4, HD]), ALU.mult).then_inc(attn_scaled, 1)
            dve.wait_ge(bo_added, TT // 2)

            def ln1_add(c):
                for b in (2 * c, 2 * c + 1):
                    dve.wait_ge(wo_psum, b + 1)
                    nc.vector.tensor_tensor(x_tok[:, 2 * b:2 * b + 2, :], x_tok[:, 2 * b:2 * b + 2, :],
                                            ps[:, b, :].rearrange("p (a b) -> p a b", a=2), ALU.add
                                            ).then_inc(ln1_sum, 1)

            def ln1_stats(c):
                for t in range(TPC * c, TPC * (c + 1)):
                    dve.wait_ge(ln1_sum, t // 2 + 1)
                    last = nc.vector.bn_stats(stats[:, t, :], x_tok[:, t, :])
                then(last)
                for t in range(TPC * c, TPC * (c + 1)):
                    last = nc.vector.bn_aggr(mean_var[:, t, :], stats[:, t, :])
                then(last)
                if c:
                    dve.wait_ge(ln1_rstd, c)
                nc.vector.tensor_scalar(var_eps[:], mean_var[:, TPC * c:TPC * (c + 1), 1], EPS, None, ALU.add
                                        ).then_inc(ln1_var, 1)

            def ln1_mean_out(c):
                dve.wait_ge(ln1_rstd, c + 1)
                nc.vector.scalar_tensor_tensor(neg_mean[:, TPC * c:TPC * (c + 1)],
                                               mean_var[:, TPC * c:TPC * (c + 1), 0], -1.0,
                                               rstd[:, TPC * c:TPC * (c + 1)], ALU.mult, ALU.mult
                                               ).then_inc(ln1_mean, 1)

            def ln1_lo(c):
                for ko in range(KO):
                    dve.wait_ge(yt_hi_ready, KO * c + ko + 1)
                    nc.vector.tensor_tensor(yt_lo[:, ko, c * CW:(c + 1) * CW], ps[:, YT_BANK[c] + ko, :],
                                            yt_hi[:, ko, c * CW:(c + 1) * CW].bitcast(f32), ALU.subtract
                                            ).then_inc(yt_ready, 1)

            ln1_add(0)
            ln1_stats(0)
            ln1_add(1)
            ln1_mean_out(0)
            ln1_stats(1)
            ln1_add(2)
            ln1_mean_out(1)
            ln1_stats(2)
            ln1_lo(0)
            ln1_mean_out(2)
            ln1_add(3)
            ln1_stats(3)

            dve.wait_ge(scales_loaded, 16 * 3)

            def ln2_step(c, step):
                if step == 0:
                    for i in range(TPC):
                        dve.wait_ge(down_psum, c * TPC + i + 1)
                        nc.vector.tensor_tensor(r_tmp[:, i, :], ps[:, 4 + i, 0:HID], sdown_b[:], ALU.mult
                                                ).then_inc(down_free, 1)
                elif step == 1:
                    dve.wait_ge(down_free, (c + 2) * TPC)
                    nc.vector.tensor_tensor(r_tmp[:], r_tmp[:], x_tok[:, bass.ds(c * TPC, TPC), :], ALU.add
                                            ).then_inc(ln2_sum, 1)
                elif step == 2:
                    dve.wait_ge(ln2_sum, c + 1)
                    for i in range(TPC):
                        last = nc.vector.bn_stats(stats[:, i, :], r_tmp[:, i, :])
                    last.then_inc(ln2_stat, 1)
                elif step == 3:
                    dve.wait_ge(ln2_stat, c + 1)
                    dve.sem_inc(ln2_gate, 1)
                    for i in range(TPC):
                        last = nc.vector.bn_aggr(mean_var[:, i, :], stats[:, i, :])
                    last.then_inc(ln2_aggr, 1)
                    dve.wait_ge(ln2_aggr, c + 1)
                    nc.vector.tensor_scalar(var_eps[:], mean_var[:, 0:TPC, 1], EPS, None, ALU.add
                                            ).then_inc(ln2_var, 1)
                else:
                    dve.wait_ge(ln2_rstd, c + 1)
                    dve.wait_ge(stored, (c + 1) * 16)
                    for i in range(TPC):
                        nc.vector.tensor_scalar(out_tmp[:, i, :], r_tmp[:, i, :], mean_var[:, i, 0:1],
                                                rstd[:, i:i + 1], ALU.subtract, ALU.mult).then_inc(ln2_ready, 1)

            def ffn_chunk(c, first):
                for m in range(MT + 1):
                    if not first and LAG <= m < LAG + 5:
                        ln2_step(c - 1, m - LAG)
                    if m < MT:
                        u = c * MT + m
                        dve.wait_ge(silu_done, u + 1)
                        dve.wait_ge(h_ready, u + 1)
                        nc.vector.scalar_tensor_tensor(h32[:, m % 2, :], ps[:, 2 + m % 2, :], sup_c[:, m:m + 1],
                                                       sg[:, m % 2, :], ALU.mult, ALU.mult
                                                       ).then_inc(gate_up_free, 1)
                    if first and m == 0:
                        ln1_mean_out(3)
                        ln1_lo(1)
                    if m > 0:
                        dve.wait_ge(h_hi_ready, c * MT + m)
                        nc.vector.tensor_tensor(h_lo[:, m - 1, :], h32[:, (m - 1) % 2, :],
                                                h_hi[:, m - 1, :].bitcast(f32), ALU.subtract).then_inc(h_ready, 1)
                    if first and m == 1:
                        ln1_lo(2)
                    if first and m == 2:
                        ln1_lo(3)

            ffn_chunk(0, True)
            with dve.Fori(1, CH) as c:
                ffn_chunk(c, False)
            def tail_scale_down(b):
                dve.wait_ge(down_psum, (CH - 1) * TPC + 2 * b + 2)
                nc.vector.tensor_tensor(r_tmp[:, 2 * b:2 * b + 2, :], ps[:, 4 + 2 * b:6 + 2 * b, 0:HID],
                                        sdown_b[:].unsqueeze(1).to_broadcast([P, 2, HID]), ALU.mult
                                        ).then_inc(down_free, 1)

            def tail_stats(b):
                for i in range(2 * b, 2 * b + 2):
                    last = nc.vector.bn_stats(stats[:, i, :], r_tmp[:, i, :])
                last.then_inc(ln2_stat, 1)
                dve.wait_ge(ln2_stat, CH + b)
                for i in range(2 * b, 2 * b + 2):
                    last = nc.vector.bn_aggr(mean_var[:, i, :], stats[:, i, :])
                last.then_inc(ln2_aggr, 1)
                dve.wait_ge(ln2_aggr, CH + b)
                nc.vector.tensor_scalar(var_eps[:, 2 * b:2 * b + 2], mean_var[:, 2 * b:2 * b + 2, 1], EPS, None,
                                        ALU.add).then_inc(ln2_var, 1)

            tail_scale_down(0)
            tail_scale_down(1)
            dve.wait_ge(down_free, CH * TPC + 2)
            nc.vector.tensor_tensor(r_tmp[:, 2:4, :], r_tmp[:, 2:4, :], x_tok[:, TT - 2:TT, :], ALU.add
                                    ).then_inc(ln2_sum, 1)
            dve.wait_ge(tail_sum, 1)
            tail_stats(0)
            dve.wait_ge(ln2_sum, CH)
            tail_stats(1)
            dve.wait_ge(stored, CH * 16)
            for b in range(2):
                i = 2 * b
                dve.wait_ge(ln2_rstd, CH + b)
                nc.vector.scalar_tensor_tensor(neg_mean[:, i:i + 1], mean_var[:, i, 0:1], -1.0, rstd[:, i:i + 1],
                                               ALU.mult, ALU.mult).then_inc(tail_mean, 1)
                nc.vector.tensor_scalar(out_tmp[:, i + 1, :], r_tmp[:, i + 1, :], mean_var[:, i + 1, 0:1],
                                        rstd[:, i + 1:i + 2], ALU.subtract, ALU.mult).then_inc(ln2_ready, 1)

        @block.tensor
        def _(pe):
            def keep_busy(count):
                for _ in range(count):
                    nc.tensor.transpose(ps[:, WARM_BANK, 0:P], ident[:], ident[:])

            pe.wait_ge(consts_ready, 1)
            keep_busy(WARM_BEFORE)
            pe.wait_ge(consts_ready, 2)

            def turn_x(c):
                if c == 0:
                    pe.wait_ge(x_half_loaded, 16)
                else:
                    pe.wait_ge(x_loaded[c], 16)
                    pe.wait_ge(xt_ready, KO * c)
                for half in range(2):
                    if c == 0 and half == 1:
                        pe.wait_ge(x_loaded[0], 16)
                    for ko in range(KO):
                        for i in range(half * TPC // 2, (half + 1) * TPC // 2):
                            last = nc.tensor.transpose(ps[:, X_BANK + ko, i * P:(i + 1) * P],
                                                       x_tok[:, TPC * c + i, ko * P:(ko + 1) * P], ident[:])
                        if half == 1:
                            last.then_inc(xt_psum, 1)

            turn_x(0)
            keep_busy(WARM_BEHIND)

            def products(dst, hi_w, lo_w, hi_x, lo_x, first=False):
                terms = [(w, x, ko) for w, x in ((hi_w, hi_x), (hi_w, lo_x), (lo_w, hi_x)) for ko in range(KO)]
                for n, (w, x, ko) in enumerate(terms):
                    if first and n == KO:
                        pe.wait_ge(xt_ready, KO)
                        pe.wait_ge(w_ready, 1)
                    last = nc.tensor.matmul(dst, w(ko), x(ko), start=(n == 0), stop=(n == len(terms) - 1))
                return last

            def project_v(p):
                if V_BANK[p] < QK_BANKS:
                    pe.wait_ge(rest_ready, len(QK) - QK_BANKS + V_BANK[p] + 1)
                elif p >= 2:
                    pe.wait_ge(v_ready, p - 1)
                for a in range(2):
                    t = 2 * p + a
                    last = products(ps[:, V_BANK[p], a * HID:(a + 1) * HID],
                                    lambda ko: xt_hi[:, ko, t * P:(t + 1) * P],
                                    lambda ko: xt_lo[:, ko, t * P:(t + 1) * P],
                                    lambda ko: w_hi[:, 2, ko, :], lambda ko: w_lo[:, 2, ko, :])
                last.then_inc(v_psum, 1)

            for n, (c, k) in enumerate(QK):
                if n == 0:
                    pe.wait_ge(xt_hi_ready, KO)
                    pe.wait_ge(w_hi_ready, 1)
                else:
                    pe.wait_ge(xt_ready, KO * (c + 1))
                    pe.wait_ge(w_ready, 2)
                if n >= QK_BANKS:
                    pe.wait_ge(squares_ready, n - QK_BANKS + 1)
                    pe.wait_ge(rest_ready, n - QK_BANKS + 1)
                i, m = k // 2, k % 2
                products(ps[:, n % QK_BANKS, :],
                         lambda ko: w_hi[:, i, ko, m * P:(m + 1) * P], lambda ko: w_lo[:, i, ko, m * P:(m + 1) * P],
                         lambda ko: xt_hi[:, ko, c * CW:(c + 1) * CW], lambda ko: xt_lo[:, ko, c * CW:(c + 1) * CW],
                         first=(n == 0)).then_inc(proj_psum, 1)
                if n % 4 == 1 and c + 1 < CH:
                    turn_x(c + 1)
                if n % 4 == 3 and c + 1 < CH:
                    pe.wait_ge(w_ready, 3)
                    for p in V_AFTER[c]:
                        project_v(p)

            def norms(n):
                k = QK[len(QK) - 4 + n][1]
                pe.wait_ge(squares_ready, len(QK) - 3 + n)
                if n >= 2:
                    pe.wait_ge(rest_ready, len(QK) - 5 + n)
                for c in range(CH):
                    last = nc.tensor.matmul(ps[32 * c:32 * c + 32, NORM_BANK[n], :], head_sum[:],
                                            squares[:, k, c * CW:(c + 1) * CW], start=True, stop=True)
                if n % 2:
                    last.then_inc(norms_psum, 1)

            norms(0)
            norms(1)
            project_v(V_AFTER[CH - 1][0])
            norms(2)
            norms(3)
            for p in V_AFTER[CH - 1][1:]:
                project_v(p)

            pe.wait_ge(flag_ready, 1)
            need_exact = pe.value_load(exact_flag[0:1, 0:1], min_val=0, max_val=1)
            with pe.If(need_exact > 0):
                with pe.Fori(0, NH) as h:
                    pe.wait_ge(gen_loaded, (h + 1) * STACK)
                    for t in range(TT):
                        if t == 0:
                            pe.wait_ge(rest_ready, len(QK))
                            pe.wait_ge(v_ready, TT // 2)
                        pe.wait_ge(gen_max, h * TT + t + 1)
                        for b in range(CH):
                            last = nc.tensor.matmul(ps[:, 4 * (t % 2) + b, :], q_stack[0][0:SROW, t * P:(t + 1) * P],
                                                    k_stack[0][0:SROW, b * CW:(b + 1) * CW], start=True, stop=True)
                        last.then_inc(gen_scores, 1)
                pe.wait_ge(gen_max, NH * TT + 2)
                for a in range(2):
                    nc.tensor.transpose(ps[:, 0, a * P:(a + 1) * P],
                                        row_max[:].rearrange("p h (b a) -> p (h b) a", a=2)[:, :, a], ident[:]
                                        ).then_inc(gen_turned, 1)
                pe.wait_ge(bound_zero, NSLOT)
                pe.wait_ge(gen_reloaded, STACK + SHIFT)

            def prob_times_v(slot, n, kt):
                for q in range(CH):
                    last = nc.tensor.matmul(ps[32 * q:32 * q + VW, ACC, :], v_slot[slot][:, kt, :],
                                            probs[:, n % 3, q, :], start=(kt == 0), stop=(kt == TT - 1))
                last.then_inc(pv_done, 1)

            def head(h, j, i):
                slot, first = j % 3, (j == 0)
                for kt in range(TT):
                    u = h * TT + kt
                    n = j * TT + kt
                    if kt == 0:
                        pe.wait_ge(stack_loaded[slot], (i + 1 + j // 3) * (STACK + SHIFT))
                        pe.wait_ge(bound_ready, 1 if first else 2 + slot)
                    if first and kt == 2:
                        pe.wait_ge(bound_ready, 2)
                    for half in range(2):
                        ring = (2 * n + half) % 3
                        if first and kt == 0 and half == 1:
                            pe.wait_ge(rest_ready, len(QK))
                            pe.wait_ge(v_ready, TT // 2)
                        if not (first and 2 * kt + half < 3):
                            pe.wait_ge(exp_done, 2 * u + half - 2)
                        for q in (2 * half, 2 * half + 1):
                            last = nc.tensor.matmul(ps[:, 2 * ring + q % 2, :],
                                                    k_stack[slot][0:ROWS, kt * P:(kt + 1) * P],
                                                    q_stack[slot][0:ROWS, q * CW:(q + 1) * CW], start=True, stop=True)
                        last.then_inc(scores_ready, 1)
                    if kt >= 2:
                        if kt == 2:
                            pe.wait_ge(v_slot_ready, h + 1)
                            if not first:
                                pe.wait_ge(attn_saved, h)
                        pe.wait_ge(exp_done, 2 * (u - 1))
                        prob_times_v(slot, n - 2, kt - 2)
                    elif not first:
                        pe.wait_ge(exp_done, 2 * (u - 1))
                        prob_times_v((j - 1) % 3, n - 2, TT - 2 + kt)

            pe.wait_ge(ones_ready, NSLOT - 1)
            pe.wait_ge(ones_pool, 1)
            pe.wait_ge(ones_loaded, 16 * NSLOT)
            head(0, 0, 0)
            with pe.Fori(0, (NH - 1) // 3) as i:
                for j in range(1, 4):
                    head(i * 3 + j, j, i)
            for kt in (TT - 2, TT - 1):
                pe.wait_ge(exp_done, 2 * ((NH - 1) * TT + kt + 1))
                prob_times_v(0, 3 * TT + kt, kt)

            pe.wait_ge(attn_saved, NH)
            for g in range(8):
                ko, ug = g // 4, g % 4
                if g >= 4:
                    pe.wait_ge(attn_scaled, g - 3)
                for k in range(8):
                    last = nc.tensor.transpose(
                        ps[:, 2 * ug + k // 4, (k % 4) * P:(k % 4 + 1) * P],
                        attn[:, 8 * ug + k, HPB * ko:HPB * (ko + 1), :].rearrange("p r h -> p (r h)"), ident[:])
                last.then_inc(attn_turned, 1)
            def turn_y(c):
                pe.wait_ge(ln1_ready, TPC * (c + 1))
                if c in (1, 2):
                    pe.wait_ge(ln1_sum, YT_BANK[c] + KO)
                if c == 3:
                    pe.wait_ge(yt_ready, KO * 2)
                for ko in range(KO):
                    for i in range(TPC):
                        last = nc.tensor.transpose(ps[:, YT_BANK[c] + ko, i * P:(i + 1) * P],
                                                   x_tok[:, TPC * c + i, ko * P:(ko + 1) * P], ident[:])
                    last.then_inc(yt_psum, 1)

            pe.wait_ge(w_loaded[3], 16)
            steps = [(c, half, ko) for c in range(CH) for half in range(2) for ko in range(KO)]
            steps.insert(1, steps.pop(4))
            for c, half, ko in steps:
                if (c, half, ko) == (CH - 1, 0, 0):
                    turn_y(0)
                pe.wait_ge(attn_scaled, 5 + c if ko == 0 else 8)
                for b in (2 * c, 2 * c + 1):
                    last = nc.tensor.matmul(ps[:, b, half * HID:(half + 1) * HID],
                                            at32[:, ko, 2 * b + half, :, :].rearrange("p j u -> p (j u)"),
                                            wo[:, ko, :], start=(ko == 0), stop=(ko == KO - 1))
                    if ko == KO - 1 and half == 1:
                        last.then_inc(wo_psum, 1)
            turn_y(1)
            pe.wait_ge(ffn_w_ready, 3)

            def down(m):
                for i in range(TPC):
                    for j, h in enumerate((h_hi, h_lo)):
                        last = nc.tensor.matmul(ps[:, 4 + i, 0:HID], h[:, m, i * P:(i + 1) * P], wd[:, m, :],
                                                start=(m == 0 and j == 0), stop=(m == MT - 1 and j == 1))
                    if m == MT - 1:
                        last.then_inc(down_psum, 1)

            def ffn_chunk(c, first):
                for m in range(MT):
                    if first and m == 0:
                        pe.wait_ge(yt_ready, KO)
                        pe.wait_ge(ln1_sum, 4)
                    pe.wait_ge(gate_up_free, c * MT + m + 1)
                    for w, bank in ((wg, m % 2), (wu, 2 + m % 2)):
                        for ko in range(KO):
                            for j, y in enumerate((yt_hi, yt_lo)):
                                last = nc.tensor.matmul(ps[:, bank, :], w[:, ko, m * P:(m + 1) * P],
                                                        y[:, ko, bass.ds(c * CW, CW)],
                                                        start=(ko == 0 and j == 0), stop=(ko == KO - 1 and j == 1))
                    last.then_inc(gate_up_psum, 1)
                    if first and m == 0:
                        turn_y(2)
                    if first and m == 2:
                        turn_y(3)
                    if first and m == 4:
                        pe.wait_ge(yt_ready, KO * CH)
                    for b in FIRST_DOWN.get(m, ()) if first else ((m - LAG) % MT,):
                        if first:
                            pe.wait_ge(h_ready, b + 3)
                        else:
                            pe.wait_ge(h_ready, c * MT + m - LAG + 3)
                            if m == LAG:
                                pe.wait_ge(down_free, (c + 1) * TPC)
                        down(b)

            ffn_chunk(0, True)
            with pe.Fori(1, CH) as c:
                ffn_chunk(c, False)
            for m in range(MT - LAG, MT):
                pe.wait_ge(h_ready, (CH - 1) * MT + m + 3)
                down(m)


_INS = ['L0_attn_X', 'L0_attn_Wq', 'L0_attn_bq', 'L0_attn_Wk', 'L0_attn_bk', 'L0_attn_Wv', 'L0_attn_bv', 'L0_attn_Wo',
        'L0_attn_bo', 'L0_ffn_w_gate', 'L0_ffn_w_up', 'L0_ffn_w_down', 'L0_ffn_s_gate', 'L0_ffn_s_up', 'L0_ffn_s_down']


def kernel(**inputs):
    import concourse.bacc as _bacc
    from concourse.bass_utils import run_bass_kernel_spmd as _run

    nc = _bacc.Bacc("TRN2", target_bir_lowering=False, num_devices=1)
    arrays, args = {}, []
    for name in _INS:
        a = np.ascontiguousarray(inputs[name])
        if a.dtype == np.int8:
            a = a.view(np.int32)
        arrays[f"in_{name}"] = a
        args.append(nc.dram_tensor(f"in_{name}", a.shape, mybir.dt.from_np(a.dtype), kind="ExternalInput").ap())
    shape = np.shape(inputs['L0_attn_X'])
    args.append(nc.dram_tensor("out_0", shape, mybir.dt.float32, kind="ExternalOutput").ap())
    layer_program(nc, *args)
    r = _run(nc, [arrays], core_ids=[0])
    return r.results[0]["out_0"]
```
